# Optimizing a Trainium2 kernel written in Bass

```python
import numpy as np
import jax
import jax.numpy as jnp

def _softmax(x, axis=-1):
    return jax.nn.softmax(x, axis=axis)

def _gelu(x):
    return jax.nn.gelu(x, approximate=True)

def _silu(x):
    return jax.nn.silu(x)

def _sigmoid(x):
    return jax.nn.sigmoid(x)

def _layernorm(x, axis=-1, eps=1e-05):
    m = jnp.mean(x, axis=axis, keepdims=True)
    v = jnp.var(x, axis=axis, keepdims=True)
    return (x - m) / jnp.sqrt(v + eps)

def _scatter_add(tgt, idx, src, axis=0):
    return tgt.at[idx].add(src)

def _segment_sum(src, seg, n):
    return jax.ops.segment_sum(src, seg, n)
kernel_name = 'mk_macaron_d2_jaxref_r8_57f623'

def setup_inputs(seed: int=0):
    np.random.seed(seed)
    _w = jnp.asarray

    def _L0_attn_setup():
        import jax, jax.numpy as jnp
        import numpy as np
        D_MODEL = 128
        D_STATE = 16
        EXPAND = 2
        D_INNER = D_MODEL * EXPAND
        DT_RANK = (D_MODEL + 15) // 16
        BATCH = 2
        SEQ = 128

        def _s6_forward(x, W_in, W_conv, W_x, W_dt, b_dt, A_log, D_param, W_out):
            B, L, _ = x.shape
            u, res = jnp.split(x @ W_in, 2, axis=-1)
            up = jnp.pad(u, ((0, 0), (2, 0), (0, 0)))
            u = up[:, :L] * W_conv[:, 0] + up[:, 1:L + 1] * W_conv[:, 1] + up[:, 2:L + 2] * W_conv[:, 2]
            u = jax.nn.silu(u)
            x_dbl = u @ W_x
            dt, Bm, Cm = jnp.split(x_dbl, [DT_RANK, DT_RANK + D_STATE], axis=-1)
            delta = jax.nn.softplus(dt @ W_dt + b_dt)
            A = -jnp.exp(A_log)
            deltaA = jnp.exp(jnp.einsum('bld,dn->bldn', delta, A))
            deltaB_u = jnp.einsum('bld,bln->bldn', delta * u, Bm)

            def step(h, inp):
                dA, dbu, c = inp
                h = dA * h + dbu
                y = jnp.einsum('bdn,bn->bd', h, c)
                return (h, y)
            h0 = jnp.zeros((B, D_INNER, D_STATE), dtype=u.dtype)
            _, ys = jax.lax.scan(step, h0, (jnp.moveaxis(deltaA, 1, 0), jnp.moveaxis(deltaB_u, 1, 0), jnp.moveaxis(Cm, 1, 0)))
            y = jnp.moveaxis(ys, 0, 1)
            y = y + u * D_param
            y = y * jax.nn.silu(res)
            return y @ W_out
        key = jax.random.key(seed)
        ks = jax.random.split(key, 8)

        def nrm(k, shape, scale):
            return jax.random.normal(k, shape, dtype=jnp.float32) * scale
        x = jax.random.normal(ks[0], (BATCH, SEQ, D_MODEL), dtype=jnp.float32)
        W_in = nrm(ks[1], (D_MODEL, 2 * D_INNER), D_MODEL ** (-0.5))
        W_conv = nrm(ks[2], (D_INNER, 3), 3 ** (-0.5))
        W_x = nrm(ks[3], (D_INNER, DT_RANK + 2 * D_STATE), D_INNER ** (-0.5))
        W_dt = nrm(ks[4], (DT_RANK, D_INNER), DT_RANK ** (-0.5))
        b_dt = nrm(ks[5], (D_INNER,), 0.1)
        A_log = jnp.log(jnp.tile(jnp.arange(1, D_STATE + 1, dtype=jnp.float32), (D_INNER, 1)))
        D_param = jnp.ones((D_INNER,), dtype=jnp.float32)
        W_out = nrm(ks[6], (D_INNER, D_MODEL), D_INNER ** (-0.5))
        return {'x': x, 'W_in': W_in, 'W_conv': W_conv, 'W_x': W_x, 'W_dt': W_dt, 'b_dt': b_dt, 'A_log': A_log, 'D_param': D_param, 'W_out': W_out}
    _L0_attn_in = _L0_attn_setup()

    def _L0_ffn_setup():
        import jax, jax.numpy as jnp
        import numpy as np
        B, T, C = (2, 256, 128)
        E, F = (8, 128)
        FS = 256
        TOP_K = 2
        key = jax.random.key(seed)
        ks = jax.random.split(key, 6)
        s = lambda *d: 1.0 / np.sqrt(d[-1])
        return {'hidden_tensor': jax.random.normal(ks[0], (B, T, C), jnp.float32), 'w_router': jax.random.normal(ks[1], (E, C), jnp.float32) * s(C), 'w1_stack': jax.random.normal(ks[2], (E, F, C), jnp.float32) * s(C), 'w2_stack': jax.random.normal(ks[3], (E, C, F), jnp.float32) * s(F), 'ws1': jax.random.normal(ks[4], (FS, C), jnp.float32) * s(C), 'ws2': jax.random.normal(ks[5], (C, FS), jnp.float32) * s(FS)}
    _L0_ffn_in = _L0_ffn_setup()

    def _L1_attn_setup():
        import jax, jax.numpy as jnp
        import numpy as np
        EMBED_DIM = 128
        NUM_HEADS = 16
        HEAD_DIM = EMBED_DIM // NUM_HEADS
        WL_CHANNELS = 16
        BATCH = 1
        SEQ = 128
        KERR = 2.7e-18 * 1000000.0
        SCALE = 1.0 / np.sqrt(HEAD_DIM)
        W_INIT = 0.02
        key = jax.random.key(seed)
        ks = jax.random.split(key, 7)
        x = jax.random.normal(ks[0], (BATCH, SEQ, EMBED_DIM), dtype=jnp.float32)
        Wq = jax.random.normal(ks[1], (EMBED_DIM, EMBED_DIM), dtype=jnp.float32) * W_INIT
        Wk = jax.random.normal(ks[2], (EMBED_DIM, EMBED_DIM), dtype=jnp.float32) * W_INIT
        Wv = jax.random.normal(ks[3], (EMBED_DIM, EMBED_DIM), dtype=jnp.float32) * W_INIT
        Wo = jax.random.normal(ks[4], (EMBED_DIM, EMBED_DIM), dtype=jnp.float32) * W_INIT
        bq = jnp.zeros((EMBED_DIM,), jnp.float32)
        bk = jnp.zeros((EMBED_DIM,), jnp.float32)
        bv = jnp.zeros((EMBED_DIM,), jnp.float32)
        bo = jnp.zeros((EMBED_DIM,), jnp.float32)
        phase_modulators = jax.random.normal(ks[5], (WL_CHANNELS, NUM_HEADS), dtype=jnp.float32)
        interference_weights = jnp.ones((WL_CHANNELS,), jnp.float32)
        return {'x': x, 'Wq': Wq, 'bq': bq, 'Wk': Wk, 'bk': bk, 'Wv': Wv, 'bv': bv, 'Wo': Wo, 'bo': bo, 'phase_modulators': phase_modulators, 'interference_weights': interference_weights}
    _L1_attn_in = _L1_attn_setup()

    def _L1_ffn_setup():
        import jax, jax.numpy as jnp
        import numpy as np
        CAPACITY_FACTOR = 1.25
        key = jax.random.key(seed)
        ks = jax.random.split(key, 6)
        B, S, H, E = (4, 512, 128, 8)
        scale = 1.0 / np.sqrt(H)
        return {'tokens': jax.random.normal(ks[0], (B, S, H), dtype=jnp.float32), 'gate_w': jax.random.normal(ks[1], (E, H), dtype=jnp.float32) * scale, 'w1': jax.random.normal(ks[2], (E, H, H), dtype=jnp.float32) * scale, 'b1': jax.random.normal(ks[3], (E, H), dtype=jnp.float32) * 0.01, 'w2': jax.random.normal(ks[4], (E, H, H), dtype=jnp.float32) * scale, 'b2': jax.random.normal(ks[5], (E, H), dtype=jnp.float32) * 0.01}
    _L1_ffn_in = _L1_ffn_setup()
    _d = {'L0_attn_x': _L0_attn_in['x'], 'L0_attn_W_in': _L0_attn_in['W_in'], 'L0_attn_W_conv': _L0_attn_in['W_conv'], 'L0_attn_W_x': _L0_attn_in['W_x'], 'L0_attn_W_dt': _L0_attn_in['W_dt'], 'L0_attn_b_dt': _L0_attn_in['b_dt'], 'L0_attn_A_log': _L0_attn_in['A_log'], 'L0_attn_D_param': _L0_attn_in['D_param'], 'L0_attn_W_out': _L0_attn_in['W_out'], 'L0_ffn_w_router': _L0_ffn_in['w_router'], 'L0_ffn_w1_stack': _L0_ffn_in['w1_stack'], 'L0_ffn_w2_stack': _L0_ffn_in['w2_stack'], 'L0_ffn_ws1': _L0_ffn_in['ws1'], 'L0_ffn_ws2': _L0_ffn_in['ws2'], 'L1_attn_Wq': _L1_attn_in['Wq'], 'L1_attn_bq': _L1_attn_in['bq'], 'L1_attn_Wk': _L1_attn_in['Wk'], 'L1_attn_bk': _L1_attn_in['bk'], 'L1_attn_Wv': _L1_attn_in['Wv'], 'L1_attn_bv': _L1_attn_in['bv'], 'L1_attn_Wo': _L1_attn_in['Wo'], 'L1_attn_bo': _L1_attn_in['bo'], 'L1_attn_phase_modulators': _L1_attn_in['phase_modulators'], 'L1_attn_interference_weights': _L1_attn_in['interference_weights'], 'L1_ffn_gate_w': _L1_ffn_in['gate_w'], 'L1_ffn_w1': _L1_ffn_in['w1'], 'L1_ffn_b1': _L1_ffn_in['b1'], 'L1_ffn_w2': _L1_ffn_in['w2'], 'L1_ffn_b2': _L1_ffn_in['b2']}
    _x0 = _d['L0_attn_x']
    _d['L0_attn_x'] = jax.random.normal(jax.random.fold_in(jax.random.key(seed), 1), (4, 1024, 128), dtype=_x0.dtype)
    del _x0
    return _d

def reference(L0_attn_x, L0_attn_W_in, L0_attn_W_conv, L0_attn_W_x, L0_attn_W_dt, L0_attn_b_dt, L0_attn_A_log, L0_attn_D_param, L0_attn_W_out, L0_ffn_w_router, L0_ffn_w1_stack, L0_ffn_w2_stack, L0_ffn_ws1, L0_ffn_ws2, L1_attn_Wq, L1_attn_bq, L1_attn_Wk, L1_attn_bk, L1_attn_Wv, L1_attn_bv, L1_attn_Wo, L1_attn_bo, L1_attn_phase_modulators, L1_attn_interference_weights, L1_ffn_gate_w, L1_ffn_w1, L1_ffn_b1, L1_ffn_w2, L1_ffn_b2):

    def _L0_attn_ref(x, W_in, W_conv, W_x, W_dt, b_dt, A_log, D_param, W_out):
        import jax, jax.numpy as jnp
        import numpy as np
        D_MODEL = 128
        D_STATE = 16
        EXPAND = 2
        D_INNER = D_MODEL * EXPAND
        DT_RANK = (D_MODEL + 15) // 16
        BATCH = 2
        SEQ = 128

        def _s6_forward(x, W_in, W_conv, W_x, W_dt, b_dt, A_log, D_param, W_out):
            B, L, _ = x.shape
            u, res = jnp.split(x @ W_in, 2, axis=-1)
            up = jnp.pad(u, ((0, 0), (2, 0), (0, 0)))
            u = up[:, :L] * W_conv[:, 0] + up[:, 1:L + 1] * W_conv[:, 1] + up[:, 2:L + 2] * W_conv[:, 2]
            u = jax.nn.silu(u)
            x_dbl = u @ W_x
            dt, Bm, Cm = jnp.split(x_dbl, [DT_RANK, DT_RANK + D_STATE], axis=-1)
            delta = jax.nn.softplus(dt @ W_dt + b_dt)
            A = -jnp.exp(A_log)
            deltaA = jnp.exp(jnp.einsum('bld,dn->bldn', delta, A))
            deltaB_u = jnp.einsum('bld,bln->bldn', delta * u, Bm)

            def step(h, inp):
                dA, dbu, c = inp
                h = dA * h + dbu
                y = jnp.einsum('bdn,bn->bd', h, c)
                return (h, y)
            h0 = jnp.zeros((B, D_INNER, D_STATE), dtype=u.dtype)
            _, ys = jax.lax.scan(step, h0, (jnp.moveaxis(deltaA, 1, 0), jnp.moveaxis(deltaB_u, 1, 0), jnp.moveaxis(Cm, 1, 0)))
            y = jnp.moveaxis(ys, 0, 1)
            y = y + u * D_param
            y = y * jax.nn.silu(res)
            return y @ W_out
        return _s6_forward(x, W_in, W_conv, W_x, W_dt, b_dt, A_log, D_param, W_out)

    def _L0_ffn_ref(hidden_tensor, w_router, w1_stack, w2_stack, ws1, ws2):
        import jax, jax.numpy as jnp
        import numpy as np
        B, T, C = (2, 256, 128)
        E, F = (8, 128)
        FS = 256
        TOP_K = 2
        Bb, Tt, Cc = hidden_tensor.shape
        x = hidden_tensor.reshape(-1, Cc)
        t = x.shape[0]
        logits = x @ w_router.T
        probs = jax.nn.softmax(logits, axis=-1)
        expert_weight, expert_idx = jax.lax.top_k(probs, TOP_K)
        expert_weight = expert_weight / jnp.sum(expert_weight, axis=-1, keepdims=True)
        flat_e = expert_idx.reshape(-1)
        order = jnp.argsort(flat_e, stable=True)
        sorted_e = flat_e[order]
        flat_tok = jnp.repeat(jnp.arange(t), TOP_K)
        sorted_tok = flat_tok[order]
        sorted_w = expert_weight.reshape(-1)[order]
        counts = jnp.bincount(sorted_e, length=E)
        offsets = jnp.concatenate([jnp.zeros((1,), counts.dtype), jnp.cumsum(counts)])
        local_pos = jnp.arange(t * TOP_K) - offsets[sorted_e]
        cap = t * TOP_K
        binned = jnp.zeros((E, cap, Cc), x.dtype).at[sorted_e, local_pos].set(x[sorted_tok])
        inter = jnp.einsum('ecd,efd->ecf', binned, w1_stack)
        inter = jnp.square(jax.nn.relu(inter))
        outb = jnp.einsum('ecf,edf->ecd', inter, w2_stack)
        flat_out = outb[sorted_e, local_pos] * sorted_w[:, None]
        moe_out = jnp.zeros((t, Cc), x.dtype).at[sorted_tok].add(flat_out)
        moe_out = moe_out.reshape(Bb, Tt, Cc)
        sh = jnp.square(jax.nn.relu(jnp.einsum('btc,fc->btf', hidden_tensor, ws1)))
        shared_out = jnp.einsum('btf,cf->btc', sh, ws2)
        return shared_out + moe_out

    def _L1_attn_ref(x, Wq, bq, Wk, bk, Wv, bv, Wo, bo, phase_modulators, interference_weights):
        import jax, jax.numpy as jnp
        import numpy as np
        EMBED_DIM = 128
        NUM_HEADS = 16
        HEAD_DIM = EMBED_DIM // NUM_HEADS
        WL_CHANNELS = 16
        BATCH = 1
        SEQ = 128
        KERR = 2.7e-18 * 1000000.0
        SCALE = 1.0 / np.sqrt(HEAD_DIM)
        W_INIT = 0.02
        B, S, E = x.shape
        H, D = (NUM_HEADS, HEAD_DIM)

        def proj(W, b):
            y = jnp.einsum('bse,ef->bsf', x, W) + b
            return y.reshape(B, S, H, D).transpose(0, 2, 1, 3)
        Q = proj(Wq, bq)
        K = proj(Wk, bk)
        V = proj(Wv, bv)
        cos_pm = jnp.cos(phase_modulators)

        def wl_step(acc, wl):
            cpm, iw = wl
            m = cpm[None, :, None, None]
            Qw = Q * m
            Kw = K * m
            scores = jnp.einsum('bhqd,bhkd->bhqk', Qw, Kw) * SCALE
            scores = scores * jnp.cos(KERR * scores * scores)
            attn = jax.nn.softmax(scores, axis=-1)
            out = jnp.einsum('bhqk,bhkd->bhqd', attn, V)
            return (acc + out * iw, None)
        acc0 = jnp.zeros((B, H, S, D), x.dtype)
        acc, _ = jax.lax.scan(wl_step, acc0, (cos_pm, interference_weights))
        combined = acc / WL_CHANNELS
        combined = combined.transpose(0, 2, 1, 3).reshape(B, S, E)
        return jnp.einsum('bse,ef->bsf', combined, Wo) + bo

    def _L1_ffn_ref(tokens, gate_w, w1, b1, w2, b2):
        import jax, jax.numpy as jnp
        import numpy as np
        CAPACITY_FACTOR = 1.25
        B, S, H = tokens.shape
        E = gate_w.shape[0]
        N = B * S
        cap = int(CAPACITY_FACTOR * N / E)
        x = tokens.reshape(N, H)
        probs = jax.nn.softmax(x @ gate_w.T, axis=-1)
        top2_w, top2_idx = jax.lax.top_k(probs, 2)
        a_e = top2_idx.reshape(-1)
        a_w = top2_w.reshape(-1)
        tok_id = jnp.arange(2 * N) // 2
        counts = jnp.bincount(a_e, length=E)
        keep = counts <= cap
        valid = keep[a_e]
        onehot = jax.nn.one_hot(a_e, E, dtype=jnp.int32)
        pos = jnp.take_along_axis(jnp.cumsum(onehot, axis=0) - 1, a_e[:, None], axis=1)[:, 0]
        p = jnp.where(valid, jnp.minimum(pos, cap - 1), cap)
        x_a = x[tok_id]
        buf = jnp.zeros((E, cap + 1, H), dtype=x.dtype).at[a_e, p].set(x_a)
        h = jax.nn.silu(jnp.einsum('ech,efh->ecf', buf, w1) + b1[:, None, :])
        y = jnp.einsum('ecf,egf->ecg', h, w2) + b2[:, None, :]
        contrib = y[a_e, p] * (a_w * valid.astype(x.dtype))[:, None]
        out = contrib.reshape(N, 2, H).sum(axis=1)
        return out.reshape(B, S, H)
    x = L0_attn_x
    x = x + 0.5 * _L0_ffn_ref(_layernorm(x, axis=-1), L0_ffn_w_router, L0_ffn_w1_stack, L0_ffn_w2_stack, L0_ffn_ws1, L0_ffn_ws2)
    x = x + _L0_attn_ref(_layernorm(x, axis=-1), L0_attn_W_in, L0_attn_W_conv, L0_attn_W_x, L0_attn_W_dt, L0_attn_b_dt, L0_attn_A_log, L0_attn_D_param, L0_attn_W_out)
    x = x + 0.5 * _L0_ffn_ref(_layernorm(x, axis=-1), L0_ffn_w_router, L0_ffn_w1_stack, L0_ffn_w2_stack, L0_ffn_ws1, L0_ffn_ws2)
    x = x + 0.5 * _L1_ffn_ref(_layernorm(x, axis=-1), L1_ffn_gate_w, L1_ffn_w1, L1_ffn_b1, L1_ffn_w2, L1_ffn_b2)
    x = x + _L1_attn_ref(_layernorm(x, axis=-1), L1_attn_Wq, L1_attn_bq, L1_attn_Wk, L1_attn_bk, L1_attn_Wv, L1_attn_bv, L1_attn_Wo, L1_attn_bo, L1_attn_phase_modulators, L1_attn_interference_weights)
    x = x + 0.5 * _L1_ffn_ref(_layernorm(x, axis=-1), L1_ffn_gate_w, L1_ffn_w1, L1_ffn_b1, L1_ffn_w2, L1_ffn_b2)
    return x

_drawn_inputs = setup_inputs


def setup_inputs(seed=0):
    import zlib

    import numpy as np

    out = dict(_drawn_inputs(seed))
    spreads = {'L0_attn_D_param': (1.0, 0.2),
     'L1_attn_bq': (0.0, 0.8),
     'L1_attn_bk': (0.0, 2.0),
     'L1_attn_bv': (0.0, 0.625),
     'L1_attn_bo': (0.0, 0.1),
     'L1_attn_interference_weights': (1.0, 0.6)}
    factors = {'L1_attn_Wq': 8.0,
     'L1_attn_Wk': 8.0,
     'L1_attn_Wv': 6.736,
     'L1_attn_Wo': 3.894,
     'L1_attn_phase_modulators': 8.0,
     'L1_ffn_w1': 4.082,
     'L1_ffn_b1': 64.0,
     'L1_ffn_w2': 3.956,
     'L1_ffn_b2': 64.0}
    for name, (base, spread) in spreads.items():
        noise = np.random.default_rng([zlib.crc32(name.encode()), seed]).standard_normal(out[name].shape)
        drawn = base * np.exp(spread * noise) if base else spread * noise
        out[name] = jnp.asarray(drawn.astype(out[name].dtype))
    for name, factor in factors.items():
        out[name] = (out[name] * factor).astype(out[name].dtype)
    return out
```

```python
from contextlib import ExitStack, contextmanager

import concourse.bass as bass
import numpy as np
from concourse import mybir

F32 = mybir.dt.float32
I32 = mybir.dt.int32
BF16 = mybir.dt.bfloat16
ACT = mybir.ActivationFunctionType
ALU = mybir.AluOpType
AX = mybir.AxisListType
ds = bass.ds

P = 128
TILES = 32
BATCHES = 4
SEQ = 1024
BLK = 512
BLKS = TILES * P // BLK
TPB = BLK // P
BT = SEQ // P
E = 8
EPS = 1e-5
CAP = int(1.25 * TILES * P / E)
DI = 2
NS = 16
DR = 8
H = 16
D = P // H
WL = 16
HEADS = BATCHES * H
SCALE = 1.0 / float(np.sqrt(D))
KERR = 2.7e-18 * 1000000.0
S_EXACT = 9000.0
ROUND = 12582912.0
TWO_PI_A, TWO_PI_B, TWO_PI_C = 6.28125, 0.0019350051879882812, 3.0199159819567e-07
HALF_PI = float(np.pi / 2)


class Chain:

    def __init__(self, eng, sem):
        self.eng, self.sem, self.at, self.n = eng, sem, 0, 0

    def inc(self, ins):
        self.n += 1
        ins.then_inc(self.sem, 1)
        return self.at + self.n

    def wait(self, value):
        self.eng.wait_ge(self.sem, value)

    def link(self, ins):
        self.eng.wait_ge(self.sem, self.inc(ins))

    @contextmanager
    def loop(self, trips, per):
        at, n = self.at, self.n
        with self.eng.Fori(0, trips) as i:
            self.at, self.n = at + n + i * per, 0
            yield i
            assert self.n == per, f"{self.n} operations counted, {per} stated"
        self.at, self.n = at, n + trips * per


def wait_apart(eng, sem, value, passed):
    eng.wait_ge(sem, value)
    eng.sem_inc(passed, 1)


class Scope(ExitStack):

    serial = 0

    def __init__(self, nc):
        super().__init__()
        self.nc = nc
        Scope.serial += 1
        self.tag = f"s{Scope.serial}_"
        self.sems = []

    def sb(self, name, shape, dt=F32):
        return self.enter_context(self.nc.sbuf_tensor(self.tag + name, shape, dt))

    def ps(self, name, shape):
        return self.enter_context(self.nc.psum_tensor(self.tag + name, shape, F32))

    def sem(self, name):
        self.sems.append(self.nc.alloc_semaphore(name=self.tag + name))
        return self.sems[-1]

    def __exit__(self, *exc):
        numbers = sorted(s.num for s in self.sems)
        for s in self.sems:
            self.nc.release_semaphore(s)
        while numbers:
            run = [n for i, n in enumerate(numbers) if n == numbers[0] + i]
            self.nc.gpsimd.sem_clear(range(run[0], run[-1] + 1))
            numbers = numbers[len(run):]
        return super().__exit__(*exc)


def load_tokens(nc, x_dram, x):
    with Scope(nc) as sc:
        x_loaded = sc.sem("x_loaded")
        with nc.Block() as block:
            @block.sync
            def _(sp):
                sp.dma_start(x[:, :, :], x_dram.rearrange("b (n p) c -> p (b n) c", p=P)).then_inc(x_loaded, 16)
                sp.wait_ge(x_loaded, 16)


def store_tokens(nc, x, out_dram):
    with Scope(nc) as sc:
        x_stored = sc.sem("x_stored")
        with nc.Block() as block:
            @block.sync
            def _(sp):
                sp.dma_start(out_dram.rearrange("b (n p) c -> p (b n) c", p=P), x[:, :, :]).then_inc(x_stored, 16)
                sp.wait_ge(x_stored, 16)


def make_identity(nc, ident):
    with Scope(nc) as sc:
        zeroed, made = sc.sem("zeroed"), sc.sem("made")
        with nc.Block() as block:
            @block.gpsimd
            def _(pool):
                pool.memset(ident[:, :], 0.0).then_inc(zeroed, 1)
                pool.wait_ge(zeroed, 1)
                pool.affine_select(out=ident[:, :], in_=ident[:, :], compare_op=ALU.not_equal, fill=1.0, base=0,
                                   pattern=[[-1, P]], channel_multiplier=1).then_inc(made, 1)
                pool.wait_ge(made, 1)


def normalise(nc, x, ident, xT):
    with Scope(nc) as sc:
        stats = sc.sb("stats", [P, TILES, 6])
        mean, diff, var, std, rstd = (sc.sb(n, [P, TILES]) for n in ("mean", "diff", "var", "std", "rstd"))
        xn = sc.sb("xn", [P, 2, TPB, P])
        turned = [sc.ps(f"turned{i}", [P, BLK]) for i in range(2)]
        dve_done, var_ready, std_ready = sc.sem("dve_done"), sc.sem("var_ready"), sc.sem("std_ready")
        xn_ready, xn_free, turned_ready, turned_free = (
            sc.sem(n) for n in ("xn_ready", "xn_free", "turned_ready", "turned_free"))
        with nc.Block() as block:
            @block.vector
            def _(v):
                ch = Chain(v, dve_done)
                with ch.loop(BLKS, TPB) as i:
                    for t in range(TPB):
                        ch.inc(v.bn_stats(stats[:, ds(i * TPB + t, 1), :].rearrange("p a s -> p (a s)"),
                                          x[:, ds(i * TPB + t, 1), :].rearrange("p a c -> p (a c)")))
                ch.wait(BLKS * TPB)
                ch.inc(v.tensor_tensor(diff[:, :], stats[:, :, 1], stats[:, :, 4], ALU.subtract))
                ch.inc(v.tensor_tensor(mean[:, :], stats[:, :, 1], stats[:, :, 4], ALU.add))
                ch.link(v.tensor_tensor(var[:, :], stats[:, :, 2], stats[:, :, 5], ALU.add))
                ch.inc(v.tensor_scalar(mean[:, :], mean[:, :], 0.5, None, ALU.mult))
                ch.link(v.scalar_tensor_tensor(out=diff[:, :], in0=diff[:, :], scalar=0.25, in1=diff[:, :],
                                               op0=ALU.mult, op1=ALU.mult))
                ch.link(v.scalar_tensor_tensor(out=var[:, :], in0=var[:, :], scalar=1.0 / P, in1=diff[:, :],
                                               op0=ALU.mult, op1=ALU.add))
                v.tensor_scalar(var[:, :], var[:, :], EPS, None, ALU.add).then_inc(var_ready, 1)
                v.wait_ge(std_ready, 1)
                ch.link(v.reciprocal(rstd[:, :], std[:, :]))
                with v.Fori(0, BLKS // 2) as i:
                    for slot in range(2):
                        v.wait_ge(xn_free, i * 2 + slot + 1)
                        for t in range(TPB):
                            tile = (i * 2 + slot) * TPB + t
                            ins = v.tensor_scalar(xn[:, slot, t, :],
                                                  x[:, ds(tile, 1), :].rearrange("p a c -> p (a c)"),
                                                  mean[:, ds(tile, 1)], rstd[:, ds(tile, 1)],
                                                  ALU.subtract, ALU.mult)
                        ins.then_inc(xn_ready, 1)

            @block.tensor
            def _(pe):
                pe.sem_inc(xn_free, 2)
                with pe.Fori(0, BLKS // 2) as i:
                    for slot in range(2):
                        pe.wait_ge(xn_ready, i * 2 + slot + 1)
                        pe.wait_ge(turned_free, i * 2 + slot + 1)
                        for t in range(TPB):
                            ins = pe.transpose(turned[slot][:, t * P:(t + 1) * P], xn[:, slot, t, :], ident[:, :])
                        ins.then_inc(turned_ready, 1)
                        pe.wait_ge(turned_ready, i * 2 + slot + 1)
                        pe.sem_inc(xn_free, 1)

            @block.scalar
            def _(act):
                act.sem_inc(turned_free, 2)
                act.wait_ge(var_ready, 1)
                act.activation(std[:, :], var[:, :], ACT.Sqrt).then_inc(std_ready, 1)
                with act.Fori(0, BLKS // 2) as i:
                    for slot in range(2):
                        act.wait_ge(turned_ready, i * 2 + slot + 1)
                        act.copy(xT[:, ds((i * 2 + slot) * BLK, BLK)], turned[slot][:, :]).then_inc(turned_free, 1)


def load_experts(nc, groups, ident):
    with Scope(nc) as sc:
        plain, squares = [], []
        for g, (dram, turned_sb) in enumerate(groups):
            rows, cols = dram.shape
            n, m = -(-rows // P), cols // P
            r = min(rows, P)
            buf = sc.sb(f"plain{g}", [r, n, cols])
            plain.append((buf, dram.rearrange("(n p) c -> p n c", p=r)))
            squares += [(buf[:, i, j * P:(j + 1) * P], turned_sb, i * m + j, r) for i in range(n) for j in range(m)]
        ring = [sc.ps(f"ring{i}", [P, P]) for i in range(4)]
        loaded, square_ready, square_free = sc.sem("loaded"), sc.sem("square_ready"), sc.sem("square_free")
        with nc.Block() as block:
            @block.sync
            def _(sp):
                for buf, dram in plain:
                    sp.dma_start(buf[:, :, :], dram).then_inc(loaded, 16)

            @block.tensor
            def _(pe):
                pe.wait_ge(loaded, 16 * len(plain))
                for k, (src, _, _, r) in enumerate(squares):
                    if k >= len(ring):
                        pe.wait_ge(square_free, k - len(ring) + 1)
                    pe.transpose(ring[k % len(ring)][:, 0:r], src, ident[0:r, 0:r]).then_inc(square_ready, 1)

            @block.vector
            def _(v):
                for k, (_, dst, at, r) in enumerate(squares):
                    v.wait_ge(square_ready, k + 1)
                    v.tensor_copy(dst[:, at, 0:r], ring[k % len(ring)][:, 0:r]).then_inc(square_free, 1)


def route(nc, xT, routerT, gates, b2=None, x=None, ident=None):
    capped = b2 is not None
    with Scope(nc) as sc:
        W = [P, TILES, E]
        logits = sc.ps("logits", W)
        p, first, second, tmp = (sc.sb(n, W) for n in ("p", "first", "second", "tmp"))
        top, top2, s = (sc.sb(n, [P, TILES]) for n in ("top", "top2", "s"))
        rank = sc.sb("rank", [P, E])
        counts, keep = sc.sb("counts", [P, E]), sc.sb("keep", [P, E])
        ones = sc.sb("ones", [P, P])
        total = sc.ps("total", [P, E])
        dve_done, logits_ready, shifted, exp_ready = (
            sc.sem(n) for n in ("dve_done", "logits_ready", "shifted", "exp_ready"))
        counts_ready, total_ready, gates_ready = (sc.sem(n) for n in ("counts_ready", "total_ready", "gates_ready"))
        if capped:
            b2_sb, gT = sc.sb("b2", [E, P]), sc.sb("gT", [E, BLK * BLKS])
            gT_ps = [sc.ps(f"gT_ps{i}", [E, BLK]) for i in range(2)]
            bias = [sc.ps(f"bias{i}", [P, TPB, P]) for i in range(2)]
            b2_loaded, gT_turned, gT_ready, bias_ready, bias_added = (
                sc.sem(n) for n in ("b2_loaded", "gT_turned", "gT_ready", "bias_ready", "bias_added"))

        def over(a):
            return a.unsqueeze(2).to_broadcast(W)

        with nc.Block() as block:
            @block.sync
            def _(sp):
                if capped:
                    sp.dma_start(b2_sb[:, :], b2).then_inc(b2_loaded, 16)

            @block.vector
            def _(v):
                ch = Chain(v, dve_done)
                for e in range(E):
                    ch.inc(v.memset(rank[:, e:e + 1], float(e - E)))
                ch.link(v.memset(ones[:, :], 1.0))
                v.wait_ge(logits_ready, 1)
                ch.link(v.tensor_reduce(top[:, :], logits[:, :, :], AX.X, ALU.max))
                v.tensor_tensor(tmp[:, :, :], logits[:, :, :], over(top[:, :]), ALU.subtract).then_inc(shifted, 1)
                v.wait_ge(exp_ready, 1)
                ch.link(v.tensor_reduce(s[:, :], p[:, :, :], AX.X, ALU.add))
                ch.link(v.reciprocal(s[:, :], s[:, :]))
                ch.link(v.tensor_tensor(p[:, :, :], p[:, :, :], over(s[:, :]), ALU.mult))
                rank_b = rank[:, :].unsqueeze(1).to_broadcast(W)

                def choose(values, best, chosen):
                    ch.link(v.tensor_reduce(best[:, :], values[:, :, :], AX.X, ALU.max))
                    ch.link(v.tensor_tensor(chosen[:, :, :], values[:, :, :], over(best[:, :]), ALU.is_equal))
                    ch.link(v.tensor_tensor(chosen[:, :, :], chosen[:, :, :], rank_b, ALU.mult))
                    ch.link(v.tensor_reduce(s[:, :], chosen[:, :, :], AX.X, ALU.min))
                    ch.link(v.tensor_tensor(chosen[:, :, :], chosen[:, :, :], over(s[:, :]), ALU.is_equal))

                choose(p, top, first)
                ch.link(v.scalar_tensor_tensor(out=tmp[:, :, :], in0=first[:, :, :], scalar=-4.0, in1=p[:, :, :],
                                               op0=ALU.mult, op1=ALU.add))
                choose(tmp, top2, second)
                ch.link(v.tensor_tensor(first[:, :, :], first[:, :, :], second[:, :, :], ALU.add))
                ch.link(v.tensor_tensor(p[:, :, :], p[:, :, :], first[:, :, :], ALU.mult))
                if not capped:
                    ch.link(v.tensor_tensor(s[:, :], top[:, :], top2[:, :], ALU.add))
                    ch.link(v.reciprocal(s[:, :], s[:, :]))
                    ch.link(v.tensor_scalar(s[:, :], s[:, :], 0.5, None, ALU.mult))
                    v.tensor_tensor(gates[:, :, :], p[:, :, :], over(s[:, :]), ALU.mult).then_inc(gates_ready, 1)
                    return
                v.tensor_reduce(counts[:, :], first[:, :, :].rearrange("p t e -> p e t"), AX.X,
                                ALU.add).then_inc(counts_ready, 1)
                v.wait_ge(total_ready, 1)
                ch.link(v.tensor_scalar(keep[:, :], total[:, :], float(CAP), 0.5, ALU.is_le, ALU.mult))
                v.tensor_tensor(gates[:, :, :], p[:, :, :], keep[:, :].unsqueeze(1).to_broadcast(W),
                                ALU.mult).then_inc(gates_ready, 1)
                for i in range(BLKS):
                    v.wait_ge(bias_ready, i + 1)
                    part = x[:, i * TPB:(i + 1) * TPB, :]
                    v.tensor_tensor(part, part, bias[i % 2][:, :, :], ALU.add).then_inc(bias_added, 1)

            @block.scalar
            def _(act):
                act.wait_ge(shifted, 1)
                act.activation(p[:, :, :], tmp[:, :, :], ACT.Exp).then_inc(exp_ready, 1)
                if capped:
                    for i in range(BLKS):
                        act.wait_ge(gT_turned, i + 1)
                        act.copy(gT[:, i * BLK:(i + 1) * BLK], gT_ps[i % 2][:, :]).then_inc(gT_ready, 1)

            @block.tensor
            def _(pe):
                for t in range(TILES):
                    ins = pe.matmul(logits[:, t, :], xT[:, t * P:(t + 1) * P], routerT[:, 0, 0:E],
                                    start=True, stop=True)
                ins.then_inc(logits_ready, 1)
                if not capped:
                    return
                pe.wait_ge(counts_ready, 1)
                pe.matmul(total[:, :], ones[:, :], counts[:, :], start=True, stop=True).then_inc(total_ready, 1)
                pe.wait_ge(gates_ready, 1)
                pe.wait_ge(b2_loaded, 16)
                for i in range(BLKS + 1):
                    if i < BLKS:
                        if i >= 2:
                            pe.wait_ge(gT_ready, i - 1)
                        for t in range(TPB):
                            ins = pe.transpose(gT_ps[i % 2][:, t * P:(t + 1) * P], gates[:, i * TPB + t, :],
                                               ident[:, :])
                        ins.then_inc(gT_turned, 1)
                    if i:
                        k = i - 1
                        pe.wait_ge(gT_ready, k + 1)
                        if k >= 2:
                            pe.wait_ge(bias_added, k - 1)
                        for t in range(TPB):
                            ins = pe.matmul(bias[k % 2][:, t, :], gT[:, (k * TPB + t) * P:(k * TPB + t + 1) * P],
                                            b2_sb[:, :], start=True, stop=True)
                        ins.then_inc(bias_ready, 1)


def experts(nc, x, xT, gates, w1T, w2T, b1T=None):
    shared = 0 if b1T is not None else 2
    units = E + shared
    pairs = E + shared // 2
    HR, YR = (5, 3) if shared else (4, 4)
    adds = E * TPB + shared // 2

    def added(k):
        return (k + 1) * TPB if k < E else adds

    with Scope(nc) as sc:
        hidden = [sc.ps(f"hidden{i}", [P, BLK]) for i in range(HR)]
        y = [sc.ps(f"y{i}", [P, TPB, P]) for i in range(YR)]
        relu = sc.sb("relu", [P, 2, BLK])
        act_h = sc.sb("act_h", [P, HR, BLK])
        hidden_ready, hidden_free, relu_ready, relu_free = (
            sc.sem(n) for n in ("hidden_ready", "hidden_free", "relu_ready", "relu_free"))
        act_ready, y_ready, x_added = (sc.sem(n) for n in ("act_ready", "y_ready", "x_added"))

        def wait_act_slot(eng, i, u):
            k = min((u - HR) % units, pairs - 1)
            eng.wait_ge(y_ready, i * pairs + k + 1 + (pairs if u >= HR else 0))

        with nc.Block() as block:
            @block.tensor
            def _(pe):
                pe.sem_inc(y_ready, pairs)
                with pe.Fori(0, BLKS) as i:
                    def second(k):
                        us = [k] if k < E else list(range(E, units))
                        pe.wait_ge(act_ready, i * units + us[-1] + 1)
                        pe.wait_ge(x_added, i * adds + added((k - YR) % pairs) + (adds if k >= YR else 0))
                        for t in range(TPB):
                            for u in us:
                                ins = pe.matmul(y[k % YR][:, t, :], act_h[:, u % HR, t * P:(t + 1) * P],
                                                w2T[:, u, :], start=(u == us[0]), stop=(u == us[-1]))
                        ins.then_inc(y_ready, 1)

                    for u in range(units):
                        pe.wait_ge(hidden_free, i * units + u + 1)
                        pe.matmul(hidden[u % HR][:, :], w1T[:, u, :], xT[:, ds(i * BLK, BLK)],
                                  start=True, stop=True).then_inc(hidden_ready, 1)
                        if 2 <= u < E + 2:
                            second(u - 2)
                    for k in range(units - 2, pairs):
                        second(k)

            @block.scalar
            def _(act):
                act.sem_inc(hidden_free, HR)
                with act.Fori(0, BLKS) as i:
                    for u in range(units):
                        act.wait_ge(hidden_ready, i * units + u + 1)
                        if shared:
                            act.wait_ge(relu_free, i * units + u + 1)
                            act.activation(relu[:, u % 2, :], hidden[u % HR][:, :], ACT.Relu).then_inc(relu_ready, 1)
                            act.wait_ge(relu_ready, i * units + u + 1)
                            act.sem_inc(hidden_free, 1)
                        else:
                            wait_act_slot(act, i, u)
                            act.activation(act_h[:, u % HR, :], hidden[u % HR][:, :], ACT.Silu,
                                           bias=b1T[:, u:u + 1]).then_inc(act_ready, 1)
                            act.wait_ge(act_ready, i * units + u + 1)
                            act.sem_inc(hidden_free, 1)

            @block.gpsimd
            def _(pool):
                if not shared:
                    return
                pool.sem_inc(relu_free, 2)
                with pool.Fori(0, BLKS) as i:
                    for u in range(units):
                        pool.wait_ge(relu_ready, i * units + u + 1)
                        wait_act_slot(pool, i, u)
                        r = relu[:, u % 2, :]
                        pool.tensor_tensor(act_h[:, u % HR, :], r, r, ALU.mult).then_inc(act_ready, 1)
                        pool.wait_ge(act_ready, i * units + u + 1)
                        pool.sem_inc(relu_free, 1)

            @block.vector
            def _(v):
                v.sem_inc(x_added, adds)
                with v.Fori(0, BLKS) as i:
                    for k in range(pairs):
                        v.wait_ge(y_ready, i * pairs + pairs + k + 1)
                        if k == E:
                            v.wait_ge(x_added, i * adds + adds + added(k - 1))
                            part = x[:, ds(i * TPB, TPB), :]
                            v.scalar_tensor_tensor(out=part, in0=y[k % YR][:, :, :], scalar=0.5, in1=part,
                                                   op0=ALU.mult, op1=ALU.add).then_inc(x_added, 1)
                            continue
                        for t in range(TPB):
                            if k:
                                v.wait_ge(x_added, i * adds + adds + added(k - 1) - (TPB - 1 - t))
                            part = x[:, ds(i * TPB + t, 1), :].rearrange("p a c -> p (a c)")
                            gate = gates[:, ds(i * TPB + t, 1), k:k + 1].rearrange("p a e -> p (a e)")
                            v.scalar_tensor_tensor(out=part, in0=y[k % YR][:, t, :], scalar=gate, in1=part,
                                                   op0=ALU.mult, op1=ALU.add).then_inc(x_added, 1)


def ffn0(nc, x, ident, router, w1, w2, ws1, ws2):
    with Scope(nc) as sc:
        xT, gates = sc.sb("xT", [P, TILES * P]), sc.sb("gates", [P, TILES, E])
        w1T, w2T, routerT = sc.sb("w1T", [P, E + 2, P]), sc.sb("w2T", [P, E + 2, P]), sc.sb("routerT", [P, 1, P])
        load_experts(nc, [(router, routerT[:, :, :]), (w1.rearrange("e f c -> (e f) c"), w1T[:, 0:E, :]),
                          (ws1, w1T[:, E:E + 2, :]), (w2.rearrange("e d f -> (e d) f"), w2T[:, 0:E, :]),
                          (ws2, w2T[:, E:E + 2, :])], ident)
        normalise(nc, x, ident, xT)
        route(nc, xT, routerT, gates)
        experts(nc, x, xT, gates, w1T, w2T)


def ffn1(nc, x, ident, gate_w, w1, b1, w2, b2):
    with Scope(nc) as sc:
        xT, gates = sc.sb("xT", [P, TILES * P]), sc.sb("gates", [P, TILES, E])
        w1T, w2T, routerT = sc.sb("w1T", [P, E, P]), sc.sb("w2T", [P, E, P]), sc.sb("routerT", [P, 1, P])
        b1T = sc.sb("b1T", [P, 1, P])
        load_experts(nc, [(gate_w, routerT[:, :, :]), (w1.rearrange("e f c -> (e f) c"), w1T[:, :, :]),
                          (b1, b1T[:, :, :]), (w2.rearrange("e d f -> (e d) f"), w2T[:, :, :])], ident)
        normalise(nc, x, ident, xT)
        route(nc, xT, routerT, gates, b2, x, ident)
        experts(nc, x, xT, gates, w1T, w2T, b1T[:, 0, :])


def s6(nc, x, ident, W_in, W_conv, W_x, W_dt, b_dt, A_log, D_param, W_out):
    T = TILES * P
    with Scope(nc) as sc:
        raw = sc.sb("raw", [P, DI, BATCHES, SEQ + 2])
        gate = sc.sb("gate", [P, DI, BATCHES, SEQ])
        u = sc.sb("u", [P, DI, BATCHES, SEQ])
        bc = sc.sb("bc", [3 * 2 * NS, T], BF16)
        delta = sc.sb("delta", [P, DI, BATCHES, SEQ])
        conv_w, a_neg = sc.sb("conv_w", [P, DI, 3]), sc.sb("a_neg", [P, DI, NS])
        wx, wdt = sc.sb("wx", [P, DI, DR + 2 * NS]), sc.sb("wdt", [DR, DI * P])
        wout = sc.sb("wout", [P, DI, P])
        bdt, dparam = sc.sb("bdt", [P, DI]), sc.sb("dparam", [P, DI])
        with Scope(nc) as front:
            dt = front.sb("dt", [DR, T])
            with Scope(nc) as inner:
                xT, win = inner.sb("xT", [P, T]), inner.sb("win", [P, 2 * DI * P])
                normalise(nc, x, ident, xT)
                s6_inner(nc, xT, win, W_in, W_conv, W_x, W_dt, b_dt, A_log, D_param, W_out, raw, gate, u, bc, dt,
                         conv_w, a_neg, wx, wdt, wout, bdt, dparam)
            s6_delta(nc, dt, wdt, bdt, u, delta, raw)
        s6_scan(nc, x, ident, bc, delta, raw, u, gate, a_neg, dparam, wout)


def s6_inner(nc, xT, win, W_in, W_conv, W_x, W_dt, b_dt, A_log, D_param, W_out, raw, gate, u, bc, dt, conv_w, a_neg,
             wx, wdt, wout, bdt, dparam):
    HB = SEQ // BLK
    with Scope(nc) as sc:
        conv = sc.sb("conv", [P, 2, SEQ])
        inner = [[sc.ps(f"inner{s}_{m}", [P, BLK]) for m in range(2 * DI)] for s in range(2)]
        loaded, zeroed, dve_done = sc.sem("loaded"), sc.sem("zeroed"), sc.sem("dve_done")
        inner_ready, inner_free, raw_ready, conv_ready, conv_free, u_ready, xd_ready, xd_free = (
            sc.sem(n) for n in ("inner_ready", "inner_free", "raw_ready", "conv_ready", "conv_free", "u_ready",
                                "xd_ready", "xd_free"))
        rest, mid = sc.sb("rest", [2 * NS, 2, BLK]), sc.sb("mid", [2 * NS, 2, BLK], BF16)
        act_done, dt_copied, bc_split = sc.sem("act_done"), sc.sem("dt_copied"), sc.sem("bc_split")
        loads = [(win[:, :], W_in), (conv_w[:, :, :], W_conv.rearrange("(h p) k -> p h k", p=P)),
                 (wx[:, :, :], W_x.rearrange("(h p) k -> p h k", p=P)), (wdt[:, :], W_dt),
                 (a_neg[:, :, :], A_log.rearrange("(h p) n -> p h n", p=P)),
                 (wout[:, :, :], W_out.rearrange("(h p) c -> p h c", p=P)),
                 (bdt[:, :], b_dt.rearrange("(h p) -> p h", p=P)),
                 (dparam[:, :], D_param.rearrange("(h p) -> p h", p=P))]
        with nc.Block() as block:
            @block.sync
            def _(sp):
                for dst, src in loads:
                    sp.dma_start(dst, src, allow_slow_non_contiguous=True).then_inc(loaded, 16)

            @block.tensor
            def _(pe):
                pe.wait_ge(loaded, 16 * len(loads))
                pe.sem_inc(inner_free, 2)
                with pe.Fori(0, BATCHES) as b:
                    for s in range(HB):
                        pe.wait_ge(inner_free, b * HB + s + 1)
                        for m in range(2 * DI):
                            ins = pe.matmul(inner[s][m][:, :], win[:, m * P:(m + 1) * P],
                                            xT[:, ds(b * SEQ + s * BLK, BLK)], start=True, stop=True)
                        ins.then_inc(inner_ready, 1)
                pe.wait_ge(u_ready, BATCHES * DI)
                pe.sem_inc(xd_free, 4)
                with pe.Fori(0, BATCHES) as b:
                    for s in range(HB):
                        pe.wait_ge(xd_free, (b * HB + s + 1) * 2)
                        for rows, first, last in ((DR, 0, DR), (2 * NS, DR, DR + 2 * NS)):
                            for h in range(DI):
                                ins = pe.matmul(inner[s][first // DR][0:rows, :], wx[:, h, first:last],
                                                u[:, h, ds(b, 1), s * BLK:(s + 1) * BLK]
                                                .rearrange("p a l -> p (a l)"), start=(h == 0), stop=(h == DI - 1))
                        ins.then_inc(xd_ready, 1)

            @block.scalar
            def _(act):
                ch = Chain(act, act_done)
                act.wait_ge(loaded, 16 * len(loads))
                ch.link(act.activation(a_neg[:, :, :], a_neg[:, :, :], ACT.Exp))
                ch.inc(act.activation(a_neg[:, :, :], a_neg[:, :, :], ACT.Copy, scale=-1.0))
                act.wait_ge(zeroed, 1)
                with ch.loop(BATCHES, HB * DI) as b:
                    for s in range(HB):
                        act.wait_ge(inner_ready, b * HB + s + 1)
                        for h in range(DI):
                            ins = act.copy(raw[:, h, ds(b, 1), 2 + s * BLK:2 + (s + 1) * BLK]
                                           .rearrange("p a l -> p (a l)"), inner[s][h][:, :])
                        ins.then_inc(raw_ready, 1)
                        for h in range(DI):
                            last = ch.inc(act.activation(gate[:, h, ds(b, 1), s * BLK:(s + 1) * BLK]
                                                         .rearrange("p a l -> p (a l)"), inner[s][DI + h][:, :],
                                                         ACT.Silu))
                        ch.wait(last)
                        act.sem_inc(inner_free, 1)
                with act.Fori(0, BATCHES) as b:
                    for h in range(DI):
                        act.wait_ge(conv_ready, b * DI + h + 1)
                        act.activation(u[:, h, ds(b, 1), :].rearrange("p a l -> p (a l)"), conv[:, h, :],
                                       ACT.Silu).then_inc(u_ready, 1)
                with act.Fori(0, BATCHES) as b:
                    for s in range(HB):
                        act.wait_ge(xd_ready, b * HB + s + 1)
                        act.copy(dt[:, ds(b * SEQ + s * BLK, BLK)], inner[s][0][0:DR, :]).then_inc(dt_copied, 1)
                        act.wait_ge(bc_split, b * HB + s + 1)
                        act.wait_ge(dt_copied, b * HB + s + 1)
                        act.sem_inc(xd_free, 2)

            @block.vector
            def _(v):
                ch = Chain(v, dve_done)
                v.memset(raw[:, :, :, 0:2], 0.0).then_inc(zeroed, 1)
                v.wait_ge(zeroed, 1)
                with ch.loop(BATCHES, 2 * DI) as b:
                    v.wait_ge(raw_ready, b * HB + HB)
                    v.wait_ge(conv_free, b * DI + 1)
                    for k in range(3):
                        for h in range(DI):
                            tap = raw[:, h, ds(b, 1), k:k + SEQ].rearrange("p a l -> p (a l)")
                            w = conv_w[:, h, k:k + 1]
                            if k == 0:
                                ch.inc(v.tensor_scalar(conv[:, h, :], tap, w, None, ALU.mult))
                                continue
                            ch.wait(ch.at + ch.n - 1 if k == 1 else ch.at + 2 * DI - 1 + h)
                            ins = v.scalar_tensor_tensor(out=conv[:, h, :], in0=tap, scalar=w, in1=conv[:, h, :],
                                                         op0=ALU.mult, op1=ALU.add)
                            if k == 1:
                                ch.inc(ins)
                            else:
                                ins.then_inc(conv_ready, 1)

                with ch.loop(BATCHES, HB * 4) as b:
                    for s in range(HB):
                        v.wait_ge(xd_ready, b * HB + s + 1)
                        at, src = ds(b * SEQ + s * BLK, BLK), inner[s][1][0:2 * NS, :]
                        ch.link(v.tensor_copy(bc[0:2 * NS, at], src))
                        ch.link(v.tensor_tensor(rest[:, s, :], src, bc[0:2 * NS, at], ALU.subtract))
                        ch.link(v.tensor_copy(mid[:, s, :], rest[:, s, :]))
                        ch.inc(v.tensor_copy(bc[2 * NS:4 * NS, at], mid[:, s, :]))
                        v.tensor_tensor(bc[4 * NS:6 * NS, at], rest[:, s, :], mid[:, s, :],
                                        ALU.subtract).then_inc(bc_split, 1)

            @block.gpsimd
            def _(pool):
                pool.sem_inc(conv_free, 1)
                with pool.Fori(0, BATCHES) as b:
                    pool.wait_ge(u_ready, b * DI + DI)
                    pool.sem_inc(conv_free, DI)


def s6_delta(nc, dt, wdt, bdt, u, delta, du):
    HB = SEQ // BLK
    steps = BATCHES * DI
    with Scope(nc) as sc:
        z_ps = [sc.ps(f"z{i}", [P, SEQ]) for i in range(DI)]
        z, ex, w, ln = (sc.sb(n, [P, DI, SEQ]) for n in ("z", "ex", "w", "ln"))
        z_mm, z_free, z_ready, ex_ready, w_ready, ln_ready, step_done, dve_done, act_done = (
            sc.sem(n) for n in ("z_mm", "z_free", "z_ready", "ex_ready", "w_ready", "ln_ready", "step_done",
                                "dve_done", "act_done"))
        passed = sc.sem("passed")
        with nc.Block() as block:
            @block.tensor
            def _(pe):
                pe.sem_inc(z_free, DI)
                with pe.Fori(0, BATCHES) as b:
                    for h in range(DI):
                        wait_apart(pe, z_free, b * DI + h + 1, passed)
                        for s in range(HB):
                            ins = pe.matmul(z_ps[h][:, s * BLK:(s + 1) * BLK], wdt[:, h * P:(h + 1) * P],
                                            dt[:, ds(b * SEQ + s * BLK, BLK)], start=True, stop=True)
                        ins.then_inc(z_mm, 1)

            @block.scalar
            def _(act):
                ch = Chain(act, act_done)
                act.sem_inc(step_done, DI)
                with ch.loop(BATCHES, DI) as b:
                    for h in range(DI):
                        act.wait_ge(z_mm, b * DI + h + 1)
                        act.wait_ge(step_done, b * DI + h + 1)
                        act.activation(z[:, h, :], z_ps[h][:, :], ACT.Identity,
                                       bias=bdt[:, h:h + 1]).then_inc(z_ready, 1)
                        act.wait_ge(z_ready, b * DI + h + 1)
                        act.sem_inc(z_free, 1)
                        ch.link(act.activation(ex[:, h, :], z[:, h, :], ACT.Abs))
                        act.activation(ex[:, h, :], ex[:, h, :], ACT.Exp, scale=-1.0).then_inc(ex_ready, 1)
                    for h in range(DI):
                        act.wait_ge(w_ready, b * DI + h + 1)
                        act.activation(ln[:, h, :], w[:, h, :], ACT.Ln).then_inc(ln_ready, 1)

            @block.vector
            def _(v):
                ch = Chain(v, dve_done)
                with ch.loop(BATCHES, 3 * DI) as b:
                    for h in range(DI):
                        v.wait_ge(ex_ready, b * DI + h + 1)
                        v.wait_ge(step_done, b * DI + h + 1)
                        v.tensor_scalar(w[:, h, :], ex[:, h, :], 1.0, None, ALU.add).then_inc(w_ready, 1)
                        v.wait_ge(w_ready, b * DI + h + 1)
                        ch.inc(v.scalar_tensor_tensor(out=ex[:, h, :], in0=w[:, h, :], scalar=-1.0, in1=ex[:, h, :],
                                                      op0=ALU.add, op1=ALU.subtract))
                    for h in range(DI):
                        v.wait_ge(ln_ready, b * DI + h + 1)
                        ch.link(v.tensor_tensor(ln[:, h, :], ln[:, h, :], ex[:, h, :], ALU.subtract))
                        d = delta[:, h, ds(b, 1), :].rearrange("p a l -> p (a l)")
                        ch.link(v.scalar_tensor_tensor(out=d, in0=z[:, h, :], scalar=0.0, in1=ln[:, h, :],
                                                       op0=ALU.max, op1=ALU.add))
                        v.tensor_tensor(du[:, h, ds(b, 1), 0:SEQ].rearrange("p a l -> p (a l)"), d,
                                        u[:, h, ds(b, 1), :].rearrange("p a l -> p (a l)"),
                                        ALU.mult).then_inc(step_done, 1)


def s6_scan(nc, x, ident, bc, delta, du, u, gate, a_neg, dparam, wout):
    HB = SEQ // BLK
    G = NS * DI
    R, RH = 2, 4
    with Scope(nc) as sc:
        dA, dBu = sc.sb("dA", [P, R, SEQ]), sc.sb("dBu", [P, R, SEQ])
        hs = sc.sb("hs", [P, RH, SEQ])
        sel = sc.sb("sel", [3 * 2 * NS, 2 * NS], BF16)
        b_sb = sc.sb("b_sb", [P, 2, SEQ])
        yg = sc.sb("yg", [P, DI, SEQ])
        b_ps, c_ps = sc.ps("b_ps", [P, SEQ]), sc.ps("c_ps", [P, SEQ])
        y_ps = [sc.ps(f"y_ps{h}", [P, SEQ]) for h in range(DI)]
        sel_step, passed = sc.sem("sel_step"), sc.sem("passed")
        names = ("b_ready", "b_copied", "c_ready", "dA_ready", "dBu_ready", "h_ready",
                 "hC_ready", "y_summed", "y_done", "skip_added", "yg_ready", "out_ready", "x_added")
        (b_ready, b_copied, c_ready, dA_ready, dBu_ready, h_ready, hC_ready, y_summed, y_done,
         skip_added, yg_ready, out_ready, x_added) = (sc.sem(n) for n in names)

        def slot(g):
            return g % R

        def row(t, h, b):
            return t[:, h, ds(b, 1), 0:SEQ].rearrange("p a l -> p (a l)")

        with nc.Block() as block:
            @block.gpsimd
            def _(pool):
                pool.memset(sel[:, :], 0.0).then_inc(sel_step, 1)
                for k in range(3):
                    pool.wait_ge(sel_step, k + 1)
                    pool.affine_select(out=sel[:, :], in_=sel[:, :], compare_op=ALU.not_equal, fill=1.0,
                                       base=-2 * NS * k, pattern=[[-1, 2 * NS]], channel_multiplier=1)\
                        .then_inc(sel_step, 1)
                with pool.Fori(0, BATCHES) as b:
                    for g in range(G):
                        n, h = g // DI, g % DI
                        pool.wait_ge(b_copied, b * NS + n + 1)
                        wait_apart(pool, h_ready, b * G + g - R + 1 + G, passed)
                        pool.tensor_tensor(dBu[:, slot(g), :], row(du, h, b), b_sb[:, n % 2, :],
                                           ALU.mult).then_inc(dBu_ready, 1)

            @block.scalar
            def _(act):
                with act.Fori(0, BATCHES) as b:
                    for g in range(G):
                        n, h = g // DI, g % DI
                        if h == 0:
                            act.wait_ge(b_ready, b * NS + n + 1)
                            if n >= 2:
                                act.wait_ge(dBu_ready, b * G + (n - 1) * DI)
                            act.copy(b_sb[:, n % 2, :], b_ps[:, :]).then_inc(b_copied, 1)
                        wait_apart(act, h_ready, b * G + g - R + 1 + G, passed)
                        act.activation(dA[:, slot(g), :], row(delta, h, b), ACT.Exp,
                                       scale=a_neg[:, h, n:n + 1]).then_inc(dA_ready, 1)

            @block.vector
            def _(v):
                v.sem_inc(h_ready, G)
                with v.Fori(0, BATCHES) as b:
                    def scan(g):
                        v.wait_ge(dA_ready, b * G + g + 1)
                        v.wait_ge(dBu_ready, b * G + g + 1)
                        v.wait_ge(y_summed, b * G + g - RH + 1 + G)
                        v.tensor_tensor_scan(hs[:, g % RH, :], dA[:, slot(g), :], dBu[:, slot(g), :], 0.0,
                                             ALU.mult, ALU.add).then_inc(h_ready, 1)

                    def times_c(g):
                        v.wait_ge(h_ready, b * G + G + g + 1)
                        v.wait_ge(c_ready, b * NS + g // DI + 1)
                        v.tensor_tensor(hs[:, g % RH, :], hs[:, g % RH, :], c_ps[:, :],
                                        ALU.mult).then_inc(hC_ready, 1)

                    scan(0)
                    for g in range(1, G + 1):
                        if g < G:
                            scan(g)
                        times_c(g - 1)
                    v.wait_ge(y_done, b + 1)
                    for h in range(DI):
                        v.wait_ge(out_ready, b + 1)
                        v.scalar_tensor_tensor(out=yg[:, h, :], in0=row(u, h, b), scalar=dparam[:, h:h + 1],
                                               in1=y_ps[h][:, :], op0=ALU.mult, op1=ALU.add).then_inc(skip_added, 1)
                    for h in range(DI):
                        v.wait_ge(skip_added, b * DI + h + 1)
                        v.tensor_tensor(yg[:, h, :], yg[:, h, :], row(gate, h, b), ALU.mult).then_inc(yg_ready, 1)
                    v.wait_ge(out_ready, b + 2)
                    part = x[:, ds(b * BT, BT), :].rearrange("p t c -> p (t c)")
                    v.tensor_tensor(part, part, y_ps[0][:, :], ALU.add).then_inc(x_added, 1)

            @block.tensor
            def _(pe):
                pe.wait_ge(sel_step, 4)
                pe.sem_inc(y_summed, G)
                pe.sem_inc(out_ready, 1)
                pe.sem_inc(x_added, 1)
                with pe.Fori(0, BATCHES) as b:
                    def spread(dst, m, ready):
                        for s in range(HB):
                            ins = pe.matmul(dst[:, s * BLK:(s + 1) * BLK],
                                            sel[:, m:m + 1].to_broadcast([3 * 2 * NS, P]),
                                            bc[:, ds(b * SEQ + s * BLK, BLK)], start=True, stop=True)
                        ins.then_inc(ready, 1)

                    def spread_b(n):
                        if n:
                            pe.wait_ge(b_copied, b * NS + n)
                        spread(b_ps, n, b_ready)

                    def sum_y(g):
                        n, h = g // DI, g % DI
                        pe.wait_ge(hC_ready, b * G + g + 1)
                        for s in range(HB):
                            ins = pe.matmul(y_ps[h][:, s * BLK:(s + 1) * BLK], ident[:, :],
                                            hs[:, g % RH, s * BLK:(s + 1) * BLK], start=(n == 0), stop=(n == NS - 1),
                                            skip_group_check=True)
                        ins.then_inc(y_summed, 1)

                    pe.wait_ge(x_added, b + 1)
                    spread_b(0)
                    for n in range(NS):
                        if n:
                            sum_y((n - 1) * DI)
                            pe.wait_ge(hC_ready, b * G + n * DI)
                        spread(c_ps, NS + n, c_ready)
                        if n:
                            sum_y((n - 1) * DI + 1)
                        if n + 1 < NS:
                            spread_b(n + 1)
                    sum_y(G - 2)
                    sum_y(G - 1)
                    pe.wait_ge(y_summed, b * G + 2 * G)
                    pe.sem_inc(y_done, 1)
                    pe.wait_ge(yg_ready, b * DI + DI)
                    for t in range(BT):
                        for h in range(DI):
                            ins = pe.matmul(y_ps[0][:, t * P:(t + 1) * P], yg[:, h, t * P:(t + 1) * P], wout[:, h, :],
                                            start=(h == 0), stop=(h == DI - 1))
                    ins.then_inc(out_ready, 1)


def attention(nc, x, ident, Wq, bq, Wk, bk, Wv, bv, Wo, bo, phase, interference):
    with Scope(nc) as sc:
        xT = sc.sb("xT", [P, TILES * P])
        V = sc.sb("V", [P, TILES, P])
        wq, wk, wo = (sc.sb(n, [P, P]) for n in ("wq", "wk", "wo"))
        bqh, bkh = sc.sb("bqh", [1 + D, H]), sc.sb("bkh", [1 + D, H])
        scale_w, share_w = sc.sb("scale_w", [P, WL * H]), sc.sb("share_w", [P, WL])
        bq_col, bk_col, cos_is_one = sc.sb("bq_col", [P, 1]), sc.sb("bk_col", [P, 1]), sc.sb("cos_is_one", [1, 1], I32)
        normalise(nc, x, ident, xT)
        att_setup(nc, x, xT, V, wq, wk, wo, bqh, bkh, bq_col, bk_col, scale_w, share_w, Wq, bq, Wk, bk, Wv, bv, Wo, bo, phase,
                  interference)
        att_bound(nc, ident, xT, wq, wk, bq_col, bk_col, cos_is_one)
        att_heads(nc, ident, xT, V, wq, wk, bqh, bkh, scale_w, share_w, cos_is_one)
        att_heads_cosine(nc, ident, xT, V, wq, wk, bqh, bkh, scale_w, share_w, cos_is_one)
        att_out(nc, x, ident, V, wo)


def att_setup(nc, x, xT, V, wq, wk, wo, bqh, bkh, bq_col, bk_col, scale_w, share_w, Wq, bq, Wk, bk, Wv, bv, Wo, bo, phase,
              interference):
    with Scope(nc) as sc:
        wv, bv_b, bo_b = (sc.sb(n, [P, P]) for n in ("wv", "bv_b", "bo_b"))
        turns, angle = sc.sb("turns", [P, WL * H]), sc.sb("angle", [P, WL * H])
        v_ps = [sc.ps(f"v_ps{i}", [P, TPB, P]) for i in range(2)]
        loaded, bias_zero, angle_ready, cos_ready, dve_done, v_mm, v_ready, x_ready, act_done = (
            sc.sem(n) for n in ("loaded", "bias_zero", "angle_ready", "cos_ready", "dve_done", "v_mm", "v_ready",
                                "x_ready", "act_done"))
        head_rows = "(h d) -> d h"
        loads = [(wv[:, :], Wv), (bv_b[:, :], bv.partition_broadcast(P)), (bo_b[:, :], bo.partition_broadcast(P)),
                 (scale_w[:, :], phase.rearrange("w h -> (w h)").partition_broadcast(P)),
                 (share_w[:, :], interference.partition_broadcast(P)), (wq[:, :], Wq), (wk[:, :], Wk),
                 (wo[:, :], Wo), (bqh[1:1 + D, :], bq.rearrange(head_rows, d=D)),
                 (bkh[1:1 + D, :], bk.rearrange(head_rows, d=D)), (bq_col[:, :], bq.rearrange("(p a) -> p a", a=1)),
                 (bk_col[:, :], bk.rearrange("(p a) -> p a", a=1))]
        with nc.Block() as block:
            @block.sync
            def _(sp):
                sp.wait_ge(bias_zero, 2)
                for dst, src in loads:
                    sp.dma_start(dst, src, allow_slow_non_contiguous=True).then_inc(loaded, 16)

            @block.tensor
            def _(pe):
                pe.wait_ge(loaded, 16 * len(loads))
                for i in range(BLKS):
                    if i >= 2:
                        pe.wait_ge(v_ready, i - 1)
                    for t in range(TPB):
                        ins = pe.matmul(v_ps[i % 2][:, t, :], xT[:, (i * TPB + t) * P:(i * TPB + t + 1) * P],
                                        wv[:, :], start=True, stop=True)
                    ins.then_inc(v_mm, 1)

            @block.gpsimd
            def _(pool):
                pool.wait_ge(loaded, 16 * len(loads))
                pool.tensor_tensor(x[:, :, :], x[:, :, :], bo_b[:, :].unsqueeze(1).to_broadcast([P, TILES, P]),
                                   ALU.add).then_inc(x_ready, 1)
                pool.wait_ge(x_ready, 1)

            @block.scalar
            def _(act):
                ch = Chain(act, act_done)
                act.wait_ge(angle_ready, 1)
                ch.link(act.activation(angle[:, :], angle[:, :], ACT.Sin))
                act.activation(scale_w[:, :], angle[:, :], ACT.Square).then_inc(cos_ready, 1)

            @block.vector
            def _(v):
                ch = Chain(v, dve_done)
                v.memset(bqh[:, :], 0.0).then_inc(bias_zero, 1)
                v.memset(bkh[:, :], 1.0).then_inc(bias_zero, 1)
                v.wait_ge(loaded, 16 * len(loads))
                ch.inc(v.tensor_scalar(share_w[:, :], share_w[:, :], 1.0 / WL, None, ALU.mult))
                ch.link(v.tensor_scalar(turns[:, :], scale_w[:, :], 1.0 / (2 * float(np.pi)), ROUND, ALU.mult, ALU.add))
                ch.link(v.tensor_scalar(turns[:, :], turns[:, :], ROUND, None, ALU.subtract))
                src = scale_w
                for part in (TWO_PI_A, TWO_PI_B, TWO_PI_C):
                    ch.link(v.scalar_tensor_tensor(out=angle[:, :], in0=turns[:, :], scalar=-part, in1=src[:, :],
                                                   op0=ALU.mult, op1=ALU.add))
                    src = angle
                ch.link(v.tensor_scalar(turns[:, :], angle[:, :], -1.0, None, ALU.mult))
                ch.link(v.tensor_tensor(angle[:, :], angle[:, :], turns[:, :], ALU.max))
                v.tensor_scalar(angle[:, :], angle[:, :], -1.0, HALF_PI, ALU.mult, ALU.add).then_inc(angle_ready, 1)
                v.wait_ge(cos_ready, 1)
                ch.inc(v.tensor_scalar(scale_w[:, :], scale_w[:, :], SCALE, None, ALU.mult))
                for i in range(BLKS):
                    v.wait_ge(v_mm, i + 1)
                    v.tensor_tensor(V[:, i * TPB:(i + 1) * TPB, :], v_ps[i % 2][:, :, :],
                                    bv_b[:, :].unsqueeze(1).to_broadcast([P, TPB, P]), ALU.add).then_inc(v_ready, 1)


def att_heads(nc, ident, xT, V, wq, wk, bqh, bkh, scale_w, share_w, cos_is_one):
    KT = SEQ // P
    STEPS = 2 + BT + 1 + KT
    USE_Q, USE_K, USE_S, USE_M, USE_T = 0, 1, 2, 2 + BT, 3 + BT
    M = 32
    slices = [[USE_Q, USE_K], [2], [3, 4], [5], [6], [7, 8], [9], [USE_M, USE_T]] + \
             [[USE_T + k] for k in range(1, KT)] + [[]]
    assert [u for s in slices for u in s] == list(range(STEPS)) and len(slices) == WL
    with Scope(nc) as sc:
        wqh, wkh = sc.sb("wqh", [P, 1 + D]), sc.sb("wkh", [P, 1 + D])
        Q, K = sc.sb("Q", [1 + D, SEQ]), sc.sb("K", [1 + D, SEQ])
        neg_max = sc.sb("neg_max", [P, BT])
        shifted = sc.sb("shifted", [P, 2, KT * SEQ])
        weights = sc.sb("weights", [P, 2, KT, SEQ])
        v_one = sc.sb("v_one", [P, KT, M])
        sums = sc.sb("sums", [P, 2, 2 * P])
        factor = sc.sb("factor", [P, 2, 2, 4])
        shares = sc.sb("shares", [P, WL, BT, D])
        wide = [sc.ps(f"wide{i}", [P, SEQ]) for i in range(2)]
        pv = [sc.ps(f"pv{i}", [P, 512]) for i in range(2)]
        turned = [sc.ps(f"turned{i}", [P, 2, 2, P]) for i in range(2)]
        (w_staged, v_staged, wide_ready, wide_read, exp_ready, pv_ready, sums_ready, turned_ready, turned_read,
         dve_done, pool_done, passed) = (sc.sem(n) for n in (
             "w_staged", "v_staged", "wide_ready", "wide_read", "exp_ready", "pv_ready", "sums_ready",
             "turned_ready", "turned_read", "dve_done", "pool_done", "passed"))

        def slice_of(t, n):
            return t[:, ds(n // H * BT, BT), ds(n % H * D, D)]

        with nc.Block() as block:
            @block.gpsimd
            def _(pool):
                ch = Chain(pool, pool_done)
                for w in (wqh, wkh):
                    ch.inc(pool.memset(w[:, 0:1], 0.0))
                ch.link(pool.memset(v_one[:, :, :], 0.0))
                ch.link(pool.memset(v_one[:, :, D:D + 1], 1.0))

                def stage_w(m):
                    pool.tensor_copy(wqh[:, 1:1 + D], wq[:, ds(m % H * D, D)]).then_inc(w_staged, 1)
                    pool.tensor_copy(wkh[:, 1:1 + D], wk[:, ds(m % H * D, D)]).then_inc(w_staged, 1)

                def head(n, last):
                    wait_apart(pool, pv_ready, n * WL + 2, passed)
                    pool.tensor_copy(v_one[:, :, 0:D], slice_of(V, n)).then_inc(v_staged, 1)
                    if not last:
                        wait_apart(pool, wide_ready, n * STEPS + USE_K + 1, passed)
                        stage_w(n + 1)

                with pool.If(pool.value_load(cos_is_one[:, :], min_val=0, max_val=1) > 0):
                    stage_w(0)
                    with pool.Fori(0, HEADS - 1) as n:
                        head(n, False)
                    head(HEADS - 1, True)

            @block.scalar
            def _(act):
                def head(n):
                    wait_apart(act, wide_read, n * STEPS + 2 * STEPS, passed)
                    for w in range(WL):
                        wait_apart(act, pv_ready, n * WL + w + 1, passed)
                        act.activation(weights[:, w % 2, :, :].rearrange("p k q -> p (k q)"),
                                       shifted[:, ds(n % 2, 1), :].rearrange("p a q -> p (a q)"), ACT.Exp,
                                       scale=scale_w[:, ds(n % H + w * H, 1)]).then_inc(exp_ready, 1)

                with act.If(act.value_load(cos_is_one[:, :], min_val=0, max_val=1) > 0):
                    with act.Fori(0, HEADS - 1) as n:
                        head(n)
                    head(HEADS - 1)

            @block.tensor
            def _(pe):
                def prepare(m, use):
                    bank = wide[use % 2]
                    back = {0: 0, 1: -1}.get(use, use - 1)
                    pe.wait_ge(wide_read, m * STEPS + STEPS + back)
                    if use in (USE_Q, USE_K):
                        w, count = (wqh, 1) if use == USE_Q else (wkh, 2)
                        wait_apart(pe, w_staged, m * 2 + count, passed)
                        for s in range(2):
                            ins = pe.matmul(bank[0:1 + D, s * BLK:(s + 1) * BLK], w[:, :],
                                            xT[:, ds(m // H * SEQ + s * BLK, BLK)], start=True, stop=True)
                    elif use < USE_M:
                        i = use - USE_S
                        if i == 0:
                            pe.wait_ge(wide_read, m * STEPS + STEPS + USE_K + 1)
                        for s in range(2):
                            ins = pe.matmul(bank[:, s * BLK:(s + 1) * BLK], Q[:, i * P:(i + 1) * P],
                                            K[:, s * BLK:(s + 1) * BLK], start=True, stop=True)
                    elif use == USE_M:
                        pe.wait_ge(wide_read, m * STEPS + STEPS + USE_M)
                        for i in range(BT):
                            ins = pe.matmul(bank[0:1, i * P:(i + 1) * P], neg_max[:, i:i + 1], ident[:, :],
                                            start=True, stop=True)
                    else:
                        k = use - USE_T
                        if k == 0:
                            pe.wait_ge(wide_read, m * STEPS + STEPS + USE_M + 1)
                        for s in range(2):
                            ins = pe.matmul(bank[:, s * BLK:(s + 1) * BLK], K[:, k * P:(k + 1) * P],
                                            Q[:, s * BLK:(s + 1) * BLK], start=True, stop=True)
                    ins.then_inc(wide_ready, 1)

                def turn(n, w):
                    pe.wait_ge(sums_ready, n * WL + w + 3)
                    if w % 2 == 0:
                        pe.wait_ge(turned_read, n * (WL // 2) + w // 2 + 1)
                    for c in range(2):
                        ins = pe.transpose(turned[w // 2 % 2][:, w % 2, c, :], sums[:, w % 2, c * P:(c + 1) * P],
                                           ident[:, :])
                    ins.then_inc(turned_ready, 1)

                def head(n, last):
                    for w in range(WL):
                        if w == 0:
                            pe.wait_ge(v_staged, n + 1)
                        pe.wait_ge(exp_ready, n * WL + w + 1)
                        pe.wait_ge(sums_ready, n * WL + w + 1)
                        for k in range(KT):
                            for j in range(4):
                                quarter = weights[:, w % 2, k, :].rearrange("p (c j q) -> p c j q", c=2, j=4)
                                ins = pe.matmul(pv[w % 2][M * j:M * j + M, 0:2 * P], v_one[:, k, :],
                                                quarter[:, :, j, :], start=(k == 0), stop=(k == KT - 1))
                        ins.then_inc(pv_ready, 1)
                        if w:
                            turn(n, w - 1)
                        if not last:
                            for use in slices[w]:
                                prepare(n + 1, use)
                    turn(n, WL - 1)

                with pe.If(pe.value_load(cos_is_one[:, :], min_val=0, max_val=1) > 0):
                    pe.sem_inc(pv_ready, 2)
                    pe.sem_inc(turned_ready, 2)
                    for use in range(STEPS):
                        prepare(0, use)
                    with pe.Fori(0, HEADS - 1) as n:
                        head(n, False)
                    head(HEADS - 1, True)

            @block.vector
            def _(v):
                ch = Chain(v, dve_done)

                def prepare(m, use):
                    bank = wide[use % 2]
                    v.wait_ge(wide_ready, m * STEPS + use + 1)
                    if use in (USE_Q, USE_K):
                        dst, bias = (Q, bqh) if use == USE_Q else (K, bkh)
                        ins = v.tensor_scalar(dst[:, :], bank[0:1 + D, :], bias[:, ds(m % H, 1)], None, ALU.add)
                    elif use < USE_M:
                        i = use - USE_S
                        ins = v.tensor_reduce(neg_max[:, i:i + 1], bank[:, :], AX.X, ALU.max, negate=True)
                    elif use == USE_M:
                        ins = v.tensor_copy(Q[0:1, :], bank[0:1, :])
                    else:
                        k = use - USE_T
                        ins = v.tensor_copy(shifted[:, ds(m % 2, 1), k * SEQ:(k + 1) * SEQ]
                                            .rearrange("p a q -> p (a q)"), bank[:, :])
                    ins.then_inc(wide_read, 1)

                def divide(n, pair):
                    v.wait_ge(turned_ready, n * WL + 2 * pair + 4)
                    t = turned[pair % 2][:, :, :, :].rearrange("p w c (j m) -> p (w c j) m", m=M)
                    f = factor[:, :, :, :].rearrange("p w c j -> p (w c j)")
                    ch.link(v.reciprocal(f, t[:, :, D]))
                    ch.link(v.tensor_tensor(factor[:, :, :, :].rearrange("p w c j -> p w (c j)"),
                                            factor[:, :, :, :].rearrange("p w c j -> p w (c j)"),
                                            share_w[:, 2 * pair:2 * pair + 2].unsqueeze(2).to_broadcast([P, 2, BT]),
                                            ALU.mult))
                    v.tensor_tensor(shares[:, 2 * pair:2 * pair + 2, :, :].rearrange("p w t d -> p (w t) d"),
                                    t[:, :, 0:D], f.unsqueeze(2).to_broadcast([P, 2 * BT, D]),
                                    ALU.mult).then_inc(turned_read, 1)

                def head(n, last):
                    for w in range(WL):
                        v.wait_ge(pv_ready, n * WL + w + 3)
                        v.wait_ge(turned_ready, n * WL + w + 1)
                        v.tensor_copy(sums[:, w % 2, :], pv[w % 2][:, 0:2 * P]).then_inc(sums_ready, 1)
                        if not last:
                            for use in slices[w]:
                                prepare(n + 1, use)
                        if w % 2 == 0 and w:
                            divide(n, w // 2 - 1)
                    divide(n, WL // 2 - 1)
                    v.wait_ge(turned_read, n * (WL // 2) + WL // 2 + 2)
                    ch.link(v.tensor_reduce(slice_of(V, n), shares[:, :, :, :].rearrange("p w t d -> p t d w"),
                                            AX.X, ALU.add))

                with v.If(v.value_load(cos_is_one[:, :], min_val=0, max_val=1) > 0):
                    v.sem_inc(wide_read, STEPS)
                    v.sem_inc(sums_ready, 2)
                    v.sem_inc(turned_read, 2)
                    for use in range(STEPS):
                        prepare(0, use)
                    with ch.loop(HEADS - 1, WL + 1) as n:
                        head(n, False)
                    head(HEADS - 1, True)


def att_bound(nc, ident, xT, wq, wk, bq_col, bk_col, cos_is_one):
    with Scope(nc) as sc:
        proj = [sc.ps(f"proj{i}", [P, BLK]) for i in range(2)]
        biased = sc.sb("biased", [P, 2, BLK])
        tops, top = sc.sb("tops", [P, 2, BLKS]), sc.sb("top", [P, 2])
        row, pair, bound = sc.ps("row", [1, 2, P]), sc.sb("pair", [1, 2]), sc.sb("bound", [1, 1])
        mm, biased_ready, top_taken, top_ready, row_ready, dve_done = (
            sc.sem(n) for n in ("mm", "biased_ready", "top_taken", "top_ready", "row_ready", "dve_done"))
        with nc.Block() as block:
            @block.tensor
            def _(pe):
                pe.sem_inc(biased_ready, 2)
                with pe.Fori(0, BLKS) as i:
                    for j, w in enumerate((wq, wk)):
                        pe.wait_ge(biased_ready, i * 2 + j + 1)
                        pe.matmul(proj[j][:, :], w[:, :], xT[:, ds(i * BLK, BLK)], start=True,
                                  stop=True).then_inc(mm, 1)
                pe.wait_ge(top_ready, 2)
                for j in range(2):
                    ins = pe.matmul(row[:, j, :], top[:, j:j + 1], ident[:, :], start=True, stop=True)
                ins.then_inc(row_ready, 1)

            @block.scalar
            def _(act):
                act.sem_inc(top_taken, 2)
                with act.Fori(0, BLKS) as i:
                    for j, bias in enumerate((bq_col, bk_col)):
                        act.wait_ge(mm, i * 2 + j + 1)
                        act.wait_ge(top_taken, i * 2 + j + 1)
                        act.activation(biased[:, j, :], proj[j][:, :], ACT.Identity,
                                       bias=bias[:, 0:1]).then_inc(biased_ready, 1)

            @block.vector
            def _(v):
                ch = Chain(v, dve_done)
                with v.Fori(0, BLKS) as i:
                    for j in range(2):
                        v.wait_ge(biased_ready, i * 2 + j + 3)
                        v.tensor_reduce(tops[:, j, ds(i, 1)], biased[:, j, :], AX.X, ALU.max,
                                        apply_absolute_value=True).then_inc(top_taken, 1)
                v.wait_ge(top_taken, 2 * BLKS + 2)
                for j in range(2):
                    v.tensor_reduce(top[:, j:j + 1], tops[:, j, :], AX.X, ALU.max).then_inc(top_ready, 1)
                v.wait_ge(row_ready, 1)
                ch.link(v.tensor_reduce(pair[:, :], row[:, :, :], AX.X, ALU.max))
                ch.link(v.tensor_tensor(bound[:, :], pair[:, 0:1], pair[:, 1:2], ALU.mult))
                ch.link(v.tensor_scalar(cos_is_one[:, :], bound[:, :], D * SCALE, S_EXACT, ALU.mult, ALU.is_lt))


def att_heads_cosine(nc, ident, xT, V, wq, wk, bqh, bkh, scale_w, share_w, cos_is_one):
    with Scope(nc) as sc:
        wqh, wkh, vh = sc.sb("wqh", [P, 1 + D]), sc.sb("wkh", [P, 1 + D]), sc.sb("vh", [P, BT, D])
        Q, K = sc.sb("Q", [1 + D, SEQ]), sc.sb("K", [1 + D, SEQ])
        qk, s, arg, turns, angle, cosine, ex, mix, mixT = (
            sc.sb(n, [P, SEQ]) for n in ("qk", "s", "arg", "turns", "angle", "cosine", "ex", "mix", "mixT"))
        neg_max, den = sc.sb("neg_max", [P, 1]), sc.sb("den", [P, 1])
        heads = sc.sb("heads", [P, BT, D])
        proj, s_ps, mixT_ps = (sc.ps(n, [P, SEQ]) for n in ("proj", "s_ps", "mixT_ps"))
        o_ps = sc.ps("o_ps", [P, D])
        (staged, proj_mm, qk_ready, s_mm, angle_ready, cos_ready, max_ready, exp_ready, mix_ready, mixT_mm,
         mixT_ready, o_mm, dve_done, pool_done, passed) = (sc.sem(n) for n in (
             "staged", "proj_mm", "qk_ready", "s_mm", "angle_ready", "cos_ready", "max_ready", "exp_ready",
             "mix_ready", "mixT_mm", "mixT_ready", "o_mm", "dve_done", "pool_done", "passed"))
        with nc.Block() as block:
            @block.gpsimd
            def _(pool):
                ch = Chain(pool, pool_done)
                with pool.If(pool.value_load(cos_is_one[:, :], min_val=0, max_val=1) < 1):
                    for w in (wqh, wkh):
                        ch.link(pool.memset(w[:, 0:1], 0.0))
                    with pool.Fori(0, HEADS) as n:
                        wait_apart(pool, o_mm, n * BT + BT, passed)
                        pool.tensor_copy(wqh[:, 1:1 + D], wq[:, ds(n % H * D, D)]).then_inc(staged, 1)
                        pool.tensor_copy(wkh[:, 1:1 + D], wk[:, ds(n % H * D, D)]).then_inc(staged, 1)
                        pool.tensor_copy(vh[:, :, :], V[:, ds(n // H * BT, BT), ds(n % H * D, D)]).then_inc(staged, 1)
                    pool.nop()

            @block.tensor
            def _(pe):
                with pe.If(pe.value_load(cos_is_one[:, :], min_val=0, max_val=1) < 1):
                    pe.sem_inc(o_mm, BT)
                    with pe.Fori(0, HEADS) as n:
                        for j, w in enumerate((wqh, wkh)):
                            if j:
                                pe.wait_ge(qk_ready, n * 2 + 1)
                            wait_apart(pe, staged, n * 3 + 3, passed)
                            for half in range(2):
                                ins = pe.matmul(proj[0:1 + D, half * BLK:(half + 1) * BLK], w[:, :],
                                                xT[:, ds(n // H * SEQ + half * BLK, BLK)], start=True, stop=True)
                            ins.then_inc(proj_mm, 1)
                        pe.wait_ge(qk_ready, n * 2 + 2)
                        for i in range(BT):
                            for half in range(2):
                                ins = pe.matmul(s_ps[:, half * BLK:(half + 1) * BLK], Q[:, i * P:(i + 1) * P],
                                                K[:, half * BLK:(half + 1) * BLK], start=True, stop=True)
                            ins.then_inc(s_mm, 1)
                            pe.wait_ge(mix_ready, n * BT + i + 1)
                            for k in range(BT):
                                ins = pe.transpose(mixT_ps[:, k * P:(k + 1) * P], mix[:, k * P:(k + 1) * P],
                                                   ident[:, :])
                            ins.then_inc(mixT_mm, 1)
                            pe.wait_ge(mixT_ready, n * BT + i + 1)
                            for k in range(BT):
                                ins = pe.matmul(o_ps[:, :], mixT[:, k * P:(k + 1) * P], vh[:, k, :],
                                                start=(k == 0), stop=(k == BT - 1))
                            ins.then_inc(o_mm, 1)
                    pe.nop()

            @block.scalar
            def _(act):
                with act.If(act.value_load(cos_is_one[:, :], min_val=0, max_val=1) < 1):
                    with act.Fori(0, HEADS) as n:
                        for i in range(BT):
                            with act.Fori(0, WL) as w:
                                step = (n * BT + i) * WL + w + 1
                                act.wait_ge(angle_ready, step)
                                act.activation(cosine[:, :], angle[:, :], ACT.Sin).then_inc(cos_ready, 1)
                                act.wait_ge(max_ready, step)
                                act.activation(ex[:, :], s[:, :], ACT.Exp, bias=neg_max[:, :],
                                               accum_out=den[:, :]).then_inc(exp_ready, 1)
                            act.wait_ge(mixT_mm, n * BT + i + 1)
                            act.copy(mixT[:, :], mixT_ps[:, :]).then_inc(mixT_ready, 1)
                    act.nop()

            @block.vector
            def _(v):
                ch = Chain(v, dve_done)
                TURN = 13
                with v.If(v.value_load(cos_is_one[:, :], min_val=0, max_val=1) < 1):
                    with ch.loop(HEADS, BT * (TURN * WL + 3) + 1) as n:
                        for j, (dst, bias) in enumerate(((Q, bqh), (K, bkh))):
                            v.wait_ge(proj_mm, n * 2 + j + 1)
                            v.tensor_scalar(dst[:, :], proj[0:1 + D, :], bias[:, ds(n % H, 1)], None,
                                            ALU.add).then_inc(qk_ready, 1)
                        for i in range(BT):
                            v.wait_ge(s_mm, n * BT + i + 1)
                            ch.link(v.tensor_copy(qk[:, :], s_ps[:, :]))
                            ch.link(v.memset(mix[:, :], 0.0))
                            v.sem_inc(passed, 1)
                            with ch.loop(WL, TURN) as w:
                                step = (n * BT + i) * WL + w + 1
                                ch.link(v.tensor_scalar(s[:, :], qk[:, :], scale_w[:, ds(w * H + n % H, 1)], None,
                                                        ALU.mult))
                                ch.link(v.scalar_tensor_tensor(out=arg[:, :], in0=s[:, :], scalar=KERR, in1=s[:, :],
                                                               op0=ALU.mult, op1=ALU.mult))
                                ch.link(v.tensor_scalar(turns[:, :], arg[:, :], 1.0 / (2 * float(np.pi)), ROUND,
                                                        ALU.mult, ALU.add))
                                ch.link(v.tensor_scalar(turns[:, :], turns[:, :], ROUND, None, ALU.subtract))
                                for part in (TWO_PI_A, TWO_PI_B, TWO_PI_C):
                                    ch.link(v.scalar_tensor_tensor(out=arg[:, :], in0=turns[:, :], scalar=-part,
                                                                   in1=arg[:, :], op0=ALU.mult, op1=ALU.add))
                                ch.link(v.scalar_tensor_tensor(out=turns[:, :], in0=arg[:, :], scalar=-1.0,
                                                               in1=arg[:, :], op0=ALU.mult, op1=ALU.max))
                                ch.link(v.tensor_scalar(turns[:, :], turns[:, :], float(np.pi), None, ALU.min))
                                v.tensor_scalar(angle[:, :], turns[:, :], -1.0, HALF_PI, ALU.mult,
                                                ALU.add).then_inc(angle_ready, 1)
                                v.wait_ge(cos_ready, step)
                                ch.link(v.tensor_tensor(s[:, :], s[:, :], cosine[:, :], ALU.mult))
                                v.tensor_reduce(neg_max[:, :], s[:, :], AX.X, ALU.max,
                                                negate=True).then_inc(max_ready, 1)
                                v.wait_ge(exp_ready, step)
                                ch.link(v.reciprocal(den[:, :], den[:, :]))
                                ch.link(v.tensor_tensor(den[:, :], den[:, :], share_w[:, ds(w, 1)], ALU.mult))
                                ch.link(v.scalar_tensor_tensor(out=mix[:, :], in0=ex[:, :], scalar=den[:, :],
                                                               in1=mix[:, :], op0=ALU.mult, op1=ALU.add))
                            v.sem_inc(mix_ready, 1)
                            v.wait_ge(o_mm, n * BT + i + 1 + BT)
                            ch.link(v.tensor_copy(heads[:, i, :], o_ps[:, :]))
                        ch.link(v.tensor_copy(V[:, ds(n // H * BT, BT), ds(n % H * D, D)], heads[:, :, :]))
                    v.nop()


def att_out(nc, x, ident, V, wo):
    with Scope(nc) as sc:
        turned_ps = [sc.ps(f"turned_ps{i}", [P, BLK]) for i in range(2)]
        out_ps = [sc.ps(f"out_ps{i}", [P, TPB, P]) for i in range(2)]
        turned = sc.sb("turned", [P, 2, BLK])
        turned_mm, turned_ready, out_ready, x_added = (
            sc.sem(n) for n in ("turned_mm", "turned_ready", "out_ready", "x_added"))
        with nc.Block() as block:
            @block.tensor
            def _(pe):
                for i in range(BLKS + 1):
                    if i < BLKS:
                        if i >= 2:
                            pe.wait_ge(turned_ready, i - 1)
                        for t in range(TPB):
                            ins = pe.transpose(turned_ps[i % 2][:, t * P:(t + 1) * P], V[:, i * TPB + t, :],
                                               ident[:, :])
                        ins.then_inc(turned_mm, 1)
                    if i:
                        k = i - 1
                        pe.wait_ge(turned_ready, k + 1)
                        if k >= 2:
                            pe.wait_ge(x_added, k - 1)
                        for t in range(TPB):
                            ins = pe.matmul(out_ps[k % 2][:, t, :], turned[:, k % 2, t * P:(t + 1) * P], wo[:, :],
                                            start=True, stop=True)
                        ins.then_inc(out_ready, 1)

            @block.scalar
            def _(act):
                for i in range(BLKS):
                    act.wait_ge(turned_mm, i + 1)
                    if i >= 2:
                        act.wait_ge(out_ready, i - 1)
                    act.copy(turned[:, i % 2, :], turned_ps[i % 2][:, :]).then_inc(turned_ready, 1)

            @block.vector
            def _(v):
                for i in range(BLKS):
                    v.wait_ge(out_ready, i + 1)
                    part = x[:, i * TPB:(i + 1) * TPB, :]
                    v.tensor_tensor(part, part, out_ps[i % 2][:, :, :], ALU.add).then_inc(x_added, 1)


def macaron(nc, out, L0_attn_x, L0_attn_W_in, L0_attn_W_conv, L0_attn_W_x, L0_attn_W_dt, L0_attn_b_dt, L0_attn_A_log,
            L0_attn_D_param, L0_attn_W_out, L0_ffn_w_router, L0_ffn_w1_stack, L0_ffn_w2_stack, L0_ffn_ws1, L0_ffn_ws2,
            L1_attn_Wq, L1_attn_bq, L1_attn_Wk, L1_attn_bk, L1_attn_Wv, L1_attn_bv, L1_attn_Wo, L1_attn_bo,
            L1_attn_phase_modulators, L1_attn_interference_weights, L1_ffn_gate_w, L1_ffn_w1, L1_ffn_b1, L1_ffn_w2,
            L1_ffn_b2, stages="fsfgag"):
    with Scope(nc) as sc:
        x, ident = sc.sb("x", [P, TILES, P]), sc.sb("ident", [P, P])
        make_identity(nc, ident)
        load_tokens(nc, L0_attn_x, x)
        for stage in stages:
            if stage == "f":
                ffn0(nc, x, ident, L0_ffn_w_router, L0_ffn_w1_stack, L0_ffn_w2_stack, L0_ffn_ws1, L0_ffn_ws2)
            if stage == "g":
                ffn1(nc, x, ident, L1_ffn_gate_w, L1_ffn_w1, L1_ffn_b1, L1_ffn_w2, L1_ffn_b2)
            if stage == "s":
                s6(nc, x, ident, L0_attn_W_in, L0_attn_W_conv, L0_attn_W_x, L0_attn_W_dt, L0_attn_b_dt,
                   L0_attn_A_log, L0_attn_D_param, L0_attn_W_out)
            if stage == "a":
                attention(nc, x, ident, L1_attn_Wq, L1_attn_bq, L1_attn_Wk, L1_attn_bk, L1_attn_Wv, L1_attn_bv,
                          L1_attn_Wo, L1_attn_bo, L1_attn_phase_modulators, L1_attn_interference_weights)
        store_tokens(nc, x, out)


_INS = ["L0_attn_x", "L0_attn_W_in", "L0_attn_W_conv", "L0_attn_W_x", "L0_attn_W_dt", "L0_attn_b_dt", "L0_attn_A_log",
        "L0_attn_D_param", "L0_attn_W_out", "L0_ffn_w_router", "L0_ffn_w1_stack", "L0_ffn_w2_stack", "L0_ffn_ws1",
        "L0_ffn_ws2", "L1_attn_Wq", "L1_attn_bq", "L1_attn_Wk", "L1_attn_bk", "L1_attn_Wv", "L1_attn_bv",
        "L1_attn_Wo", "L1_attn_bo", "L1_attn_phase_modulators", "L1_attn_interference_weights", "L1_ffn_gate_w",
        "L1_ffn_w1", "L1_ffn_b1", "L1_ffn_w2", "L1_ffn_b2"]


def kernel(**inputs):
    import numpy as _np
    import concourse.bacc as _bacc
    from concourse import mybir as _mybir
    from concourse.bass_utils import run_bass_kernel_spmd as _run

    nc = _bacc.Bacc("TRN2", target_bir_lowering=False, num_devices=1)
    arrays, args = {}, {}
    for name in _INS:
        a = _np.ascontiguousarray(inputs[name])
        arrays[f"in_{name}_dram"] = a
        args[name] = nc.dram_tensor(f"in_{name}_dram", a.shape, _mybir.dt.from_np(a.dtype), kind="ExternalInput").ap()
    out = nc.dram_tensor("out_0_dram", (BATCHES, SEQ, P), F32, kind="ExternalOutput").ap()
    macaron(nc, out, **args)
    r = _run(nc, [arrays], core_ids=[0])
    return r.results[0]["out_0_dram"]
```

```python
from contextlib import ExitStack, contextmanager

import concourse.bass as bass
import numpy as np
from concourse import mybir

F32 = mybir.dt.float32
I32 = mybir.dt.int32
BF16 = mybir.dt.bfloat16
ACT = mybir.ActivationFunctionType
ALU = mybir.AluOpType
AX = mybir.AxisListType
ds = bass.ds

P = 128
TILES = 32
BATCHES = 4
SEQ = 1024
BLK = 512
BLKS = TILES * P // BLK
TPB = BLK // P
BT = SEQ // P
E = 8
EPS = 1e-5
CAP = int(1.25 * TILES * P / E)
DI = 2
NS = 16
DR = 8
H = 16
D = P // H
WL = 16
HEADS = BATCHES * H
SCALE = 1.0 / float(np.sqrt(D))
KERR = 2.7e-18 * 1000000.0
S_EXACT = 9000.0
ROUND = 12582912.0
TWO_PI_A, TWO_PI_B, TWO_PI_C = 6.28125, 0.0019350051879882812, 3.0199159819567e-07
HALF_PI = float(np.pi / 2)


class Chain:

    def __init__(self, eng, sem):
        self.eng, self.sem, self.at, self.n = eng, sem, 0, 0

    def inc(self, ins):
        self.n += 1
        ins.then_inc(self.sem, 1)
        return self.at + self.n

    def wait(self, value):
        self.eng.wait_ge(self.sem, value)

    def link(self, ins):
        self.eng.wait_ge(self.sem, self.inc(ins))

    @contextmanager
    def loop(self, trips, per):
        at, n = self.at, self.n
        with self.eng.Fori(0, trips) as i:
            self.at, self.n = at + n + i * per, 0
            yield i
            assert self.n == per, f"{self.n} operations counted, {per} stated"
        self.at, self.n = at, n + trips * per


def wait_apart(eng, sem, value, passed):
    eng.wait_ge(sem, value)
    eng.sem_inc(passed, 1)


class Scope(ExitStack):

    serial = 0

    def __init__(self, nc):
        super().__init__()
        self.nc = nc
        Scope.serial += 1
        self.tag = f"s{Scope.serial}_"
        self.sems = []

    def sb(self, name, shape, dt=F32):
        return self.enter_context(self.nc.sbuf_tensor(self.tag + name, shape, dt))

    def ps(self, name, shape):
        return self.enter_context(self.nc.psum_tensor(self.tag + name, shape, F32))

    def sem(self, name):
        self.sems.append(self.nc.alloc_semaphore(name=self.tag + name))
        return self.sems[-1]

    def __exit__(self, *exc):
        numbers = sorted(s.num for s in self.sems)
        for s in self.sems:
            self.nc.release_semaphore(s)
        while numbers:
            run = [n for i, n in enumerate(numbers) if n == numbers[0] + i]
            self.nc.gpsimd.sem_clear(range(run[0], run[-1] + 1))
            numbers = numbers[len(run):]
        return super().__exit__(*exc)


def load_tokens(nc, x_dram, x):
    with Scope(nc) as sc:
        x_loaded = sc.sem("x_loaded")
        with nc.Block() as block:
            @block.sync
            def _(sp):
                sp.dma_start(x[:, :, :], x_dram.rearrange("b (n p) c -> p (b n) c", p=P)).then_inc(x_loaded, 16)
                sp.wait_ge(x_loaded, 16)


def store_tokens(nc, x, out_dram):
    with Scope(nc) as sc:
        x_stored = sc.sem("x_stored")
        with nc.Block() as block:
            @block.sync
            def _(sp):
                sp.dma_start(out_dram.rearrange("b (n p) c -> p (b n) c", p=P), x[:, :, :]).then_inc(x_stored, 16)
                sp.wait_ge(x_stored, 16)


def make_identity(nc, ident):
    with Scope(nc) as sc:
        zeroed, made = sc.sem("zeroed"), sc.sem("made")
        with nc.Block() as block:
            @block.gpsimd
            def _(pool):
                pool.memset(ident[:, :], 0.0).then_inc(zeroed, 1)
                pool.wait_ge(zeroed, 1)
                pool.affine_select(out=ident[:, :], in_=ident[:, :], compare_op=ALU.not_equal, fill=1.0, base=0,
                                   pattern=[[-1, P]], channel_multiplier=1).then_inc(made, 1)
                pool.wait_ge(made, 1)


def normalise(nc, x, ident, xT):
    with Scope(nc) as sc:
        stats = sc.sb("stats", [P, TILES, 6])
        mean, diff, var, std, rstd = (sc.sb(n, [P, TILES]) for n in ("mean", "diff", "var", "std", "rstd"))
        xn = sc.sb("xn", [P, 2, TPB, P])
        turned = [sc.ps(f"turned{i}", [P, BLK]) for i in range(2)]
        dve_done, var_ready, std_ready = sc.sem("dve_done"), sc.sem("var_ready"), sc.sem("std_ready")
        xn_ready, xn_free, turned_ready, turned_free = (
            sc.sem(n) for n in ("xn_ready", "xn_free", "turned_ready", "turned_free"))
        with nc.Block() as block:
            @block.vector
            def _(v):
                ch = Chain(v, dve_done)
                for t in range(TILES):
                    ch.inc(v.bn_stats(stats[:, t, :], x[:, t, :]))
                ch.wait(TILES)
                ch.inc(v.tensor_tensor(diff[:, :], stats[:, :, 1], stats[:, :, 4], ALU.subtract))
                ch.inc(v.tensor_tensor(mean[:, :], stats[:, :, 1], stats[:, :, 4], ALU.add))
                ch.link(v.tensor_tensor(var[:, :], stats[:, :, 2], stats[:, :, 5], ALU.add))
                ch.inc(v.tensor_scalar(mean[:, :], mean[:, :], 0.5, None, ALU.mult))
                ch.link(v.scalar_tensor_tensor(out=diff[:, :], in0=diff[:, :], scalar=0.25, in1=diff[:, :],
                                               op0=ALU.mult, op1=ALU.mult))
                ch.link(v.scalar_tensor_tensor(out=var[:, :], in0=var[:, :], scalar=1.0 / P, in1=diff[:, :],
                                               op0=ALU.mult, op1=ALU.add))
                v.tensor_scalar(var[:, :], var[:, :], EPS, None, ALU.add).then_inc(var_ready, 1)
                v.wait_ge(std_ready, 1)
                ch.link(v.reciprocal(rstd[:, :], std[:, :]))
                with v.Fori(0, BLKS // 2) as i:
                    for slot in range(2):
                        v.wait_ge(xn_free, i * 2 + slot + 1)
                        for t in range(TPB):
                            tile = (i * 2 + slot) * TPB + t
                            ins = v.tensor_scalar(xn[:, slot, t, :],
                                                  x[:, ds(tile, 1), :].rearrange("p a c -> p (a c)"),
                                                  mean[:, ds(tile, 1)], rstd[:, ds(tile, 1)],
                                                  ALU.subtract, ALU.mult)
                        ins.then_inc(xn_ready, 1)

            @block.tensor
            def _(pe):
                pe.sem_inc(xn_free, 2)
                with pe.Fori(0, BLKS // 2) as i:
                    for slot in range(2):
                        pe.wait_ge(xn_ready, i * 2 + slot + 1)
                        pe.wait_ge(turned_free, i * 2 + slot + 1)
                        for t in range(TPB):
                            ins = pe.transpose(turned[slot][:, t * P:(t + 1) * P], xn[:, slot, t, :], ident[:, :])
                        ins.then_inc(turned_ready, 1)
                        pe.wait_ge(turned_ready, i * 2 + slot + 1)
                        pe.sem_inc(xn_free, 1)

            @block.scalar
            def _(act):
                act.sem_inc(turned_free, 2)
                act.wait_ge(var_ready, 1)
                act.activation(std[:, :], var[:, :], ACT.Sqrt).then_inc(std_ready, 1)
                with act.Fori(0, BLKS // 2) as i:
                    for slot in range(2):
                        act.wait_ge(turned_ready, i * 2 + slot + 1)
                        act.copy(xT[:, ds((i * 2 + slot) * BLK, BLK)], turned[slot][:, :]).then_inc(turned_free, 1)


def normalise_and_route(nc, x, ident, xT, groups, routerT, gates, kept=None):
    capped = kept is not None
    W = [P, TILES, E]
    with Scope(nc) as sc:
        plain, squares = [], []
        for g, (dram, turned_sb) in enumerate(groups):
            rows, cols = dram.shape
            n, m = -(-rows // P), cols // P
            r = min(rows, P)
            buf = sc.sb(f"plain{g}", [r, n, cols])
            plain.append((buf, dram.rearrange("(n p) c -> p n c", p=r)))
            squares += [(buf[:, i, j * P:(j + 1) * P], turned_sb, i * m + j, r) for i in range(n) for j in range(m)]
        ring = [sc.ps(f"ring{i}", [P, P]) for i in range(4)]
        turned = [sc.ps(f"turned{i}", [P, BLK]) for i in range(2)]
        stats = sc.sb("stats", [P, TILES, 6])
        mean, diff, var, std, rstd = (sc.sb(n, [P, TILES]) for n in ("mean", "diff", "var", "std", "rstd"))
        xn = sc.sb("xn", [P, 2, TPB, P])
        logits, total = sc.ps("logits", W), sc.ps("total", [P, E])
        p, first, second, tmp = (sc.sb(n, W) for n in ("p", "first", "second", "tmp"))
        top, top2, s = (sc.sb(n, [P, TILES]) for n in ("top", "top2", "s"))
        rank, ones = sc.sb("rank", [P, E]), sc.sb("ones", [P, P])
        counts, keep, pos = sc.sb("counts", [P, E]), sc.sb("keep", [P, E]), sc.sb("pos", [1, E])
        lower, match = sc.sb("lower", [1, E, E]), sc.sb("match", [1, E, E])
        listed = sc.sb("listed", [1, 2, E])
        (router_loaded, loaded, constants, dve_done, var_ready, std_ready, xn_ready, xn_free, turned_ready, turned_free, square_ready,
         square_free, logits_ready, shifted, exp_ready, counts_ready, total_ready) = (sc.sem(n) for n in (
             "router_loaded", "loaded", "constants", "dve_done", "var_ready", "std_ready", "xn_ready", "xn_free", "turned_ready",
             "turned_free", "square_ready", "square_free", "logits_ready", "shifted", "exp_ready", "counts_ready",
             "total_ready"))

        def over(a):
            return a.unsqueeze(2).to_broadcast(W)

        with nc.Block() as block:
            @block.sync
            def _(sp):
                for k, (buf, dram) in enumerate(plain):
                    sp.dma_start(buf[:, :, :], dram).then_inc(loaded if k else router_loaded, 16)

            @block.gpsimd
            def _(pool):
                for e in range(E):
                    pool.memset(rank[:, e:e + 1], float(e - E)).then_inc(constants, 1)
                pool.memset(ones[:, :], 1.0).then_inc(constants, 1)
                pool.memset(lower[:, :, :], 0.0).then_inc(constants, 1)
                pool.wait_ge(constants, E + 2)
                for j in range(1, E):
                    pool.memset(lower[:, j, 0:j], 1.0).then_inc(constants, 1)

            @block.vector
            def _(v):
                ch = Chain(v, dve_done)
                for t in range(TILES):
                    ch.inc(v.bn_stats(stats[:, t, :], x[:, t, :]))
                ch.wait(TILES)
                ch.inc(v.tensor_tensor(diff[:, :], stats[:, :, 1], stats[:, :, 4], ALU.subtract))
                ch.inc(v.tensor_tensor(mean[:, :], stats[:, :, 1], stats[:, :, 4], ALU.add))
                ch.link(v.tensor_tensor(var[:, :], stats[:, :, 2], stats[:, :, 5], ALU.add))
                ch.inc(v.tensor_scalar(mean[:, :], mean[:, :], 0.5, None, ALU.mult))
                ch.link(v.scalar_tensor_tensor(out=diff[:, :], in0=diff[:, :], scalar=0.25, in1=diff[:, :],
                                               op0=ALU.mult, op1=ALU.mult))
                ch.link(v.scalar_tensor_tensor(out=var[:, :], in0=var[:, :], scalar=1.0 / P, in1=diff[:, :],
                                               op0=ALU.mult, op1=ALU.add))
                v.tensor_scalar(var[:, :], var[:, :], EPS, None, ALU.add).then_inc(var_ready, 1)
                v.wait_ge(std_ready, 1)
                ch.link(v.reciprocal(rstd[:, :], std[:, :]))
                with v.Fori(0, BLKS // 2) as i:
                    for slot in range(2):
                        v.wait_ge(xn_free, i * 2 + slot + 1)
                        for t in range(TPB):
                            tile = (i * 2 + slot) * TPB + t
                            ins = v.tensor_scalar(xn[:, slot, t, :],
                                                  x[:, ds(tile, 1), :].rearrange("p a c -> p (a c)"),
                                                  mean[:, ds(tile, 1)], rstd[:, ds(tile, 1)],
                                                  ALU.subtract, ALU.mult)
                        ins.then_inc(xn_ready, 1)

                v.wait_ge(logits_ready, 1)
                ch.link(v.tensor_reduce(top[:, :], logits[:, :, :], AX.X, ALU.max))
                v.tensor_tensor(tmp[:, :, :], logits[:, :, :], over(top[:, :]), ALU.subtract).then_inc(shifted, 1)
                v.wait_ge(exp_ready, 1)
                ch.link(v.tensor_reduce(s[:, :], p[:, :, :], AX.X, ALU.add))
                ch.link(v.reciprocal(s[:, :], s[:, :]))
                ch.link(v.tensor_tensor(p[:, :, :], p[:, :, :], over(s[:, :]), ALU.mult))
                v.wait_ge(constants, 2 * E + 1)
                rank_b = rank[:, :].unsqueeze(1).to_broadcast(W)

                def choose(values, best, chosen):
                    ch.link(v.tensor_reduce(best[:, :], values[:, :, :], AX.X, ALU.max))
                    ch.link(v.tensor_tensor(chosen[:, :, :], values[:, :, :], over(best[:, :]), ALU.is_equal))
                    ch.link(v.tensor_tensor(chosen[:, :, :], chosen[:, :, :], rank_b, ALU.mult))
                    ch.link(v.tensor_reduce(s[:, :], chosen[:, :, :], AX.X, ALU.min))
                    ch.link(v.tensor_tensor(chosen[:, :, :], chosen[:, :, :], over(s[:, :]), ALU.is_equal))

                choose(p, top, first)
                ch.link(v.scalar_tensor_tensor(out=tmp[:, :, :], in0=first[:, :, :], scalar=-4.0, in1=p[:, :, :],
                                               op0=ALU.mult, op1=ALU.add))
                choose(tmp, top2, second)
                ch.link(v.tensor_tensor(first[:, :, :], first[:, :, :], second[:, :, :], ALU.add))
                ch.link(v.tensor_tensor(p[:, :, :], p[:, :, :], first[:, :, :], ALU.mult))
                if not capped:
                    ch.link(v.tensor_tensor(s[:, :], top[:, :], top2[:, :], ALU.add))
                    ch.link(v.reciprocal(s[:, :], s[:, :]))
                    ch.link(v.tensor_scalar(s[:, :], s[:, :], 0.5, None, ALU.mult))
                    ch.link(v.tensor_tensor(gates[:, :, :], p[:, :, :], over(s[:, :]), ALU.mult))
                    return
                v.tensor_reduce(counts[:, :], first[:, :, :].rearrange("p t e -> p e t"), AX.X,
                                ALU.add).then_inc(counts_ready, 1)
                v.wait_ge(total_ready, 1)
                ch.link(v.tensor_scalar(keep[:, :], total[:, :], float(CAP), None, ALU.is_le))
                ch.inc(v.scalar_tensor_tensor(out=gates[:, :, :], in0=p[:, :, :], scalar=0.5,
                                              in1=keep[:, :].unsqueeze(1).to_broadcast(W), op0=ALU.mult,
                                              op1=ALU.mult))
                square = [1, E, E]
                keep_b = keep[0:1, :].unsqueeze(1).to_broadcast(square)
                ch.link(v.tensor_tensor(match[:, :, :], lower[:, :, :], keep_b, ALU.mult))
                ch.link(v.tensor_reduce(pos[:, :], match[:, :, :], AX.X, ALU.add))
                ch.link(v.tensor_scalar(pos[:, :], pos[:, :], float(E), None, ALU.subtract))
                ch.link(v.tensor_tensor(match[:, :, :], pos[:, :].unsqueeze(1).to_broadcast(square),
                                        rank[0:1, :].unsqueeze(2).to_broadcast(square), ALU.is_equal))
                ch.link(v.tensor_tensor(match[:, :, :], match[:, :, :], keep_b, ALU.mult))
                ch.link(v.tensor_reduce(listed[:, 0, :], match[:, :, :], AX.X, ALU.add))
                ch.link(v.tensor_tensor(match[:, :, :], match[:, :, :],
                                        rank[0:1, :].unsqueeze(1).to_broadcast(square), ALU.mult))
                ch.link(v.tensor_reduce(listed[:, 1, :], match[:, :, :], AX.X, ALU.add))
                ch.link(v.scalar_tensor_tensor(out=listed[:, 1, :], in0=listed[:, 0, :], scalar=float(E),
                                               in1=listed[:, 1, :], op0=ALU.mult, op1=ALU.add))
                ch.link(v.tensor_copy(kept[:, :, :], listed[:, :, :]))

            @block.tensor
            def _(pe):
                def turn_square(k):
                    src, _, _, r = squares[k]
                    if k >= len(ring):
                        pe.wait_ge(square_free, k - len(ring) + 1)
                    pe.transpose(ring[k % len(ring)][:, 0:r], src, ident[0:r, 0:r]).then_inc(square_ready, 1)

                pe.sem_inc(xn_free, 2)
                pe.wait_ge(router_loaded, 16)
                turn_square(0)
                for b in range(BLKS + 1):
                    if b < BLKS:
                        pe.wait_ge(xn_ready, b + 1)
                        pe.wait_ge(turned_free, b + 1)
                        for t in range(TPB):
                            ins = pe.transpose(turned[b % 2][:, t * P:(t + 1) * P], xn[:, b % 2, t, :], ident[:, :])
                        ins.then_inc(turned_ready, 1)
                    if b == 1:
                        pe.wait_ge(square_free, 1)
                    if b:
                        pe.wait_ge(turned_free, b + 2)
                        for t in range((b - 1) * TPB, b * TPB):
                            ins = pe.matmul(logits[:, t, :], xT[:, t * P:(t + 1) * P], routerT[:, 0, 0:E],
                                            start=True, stop=True)
                    if b < BLKS:
                        pe.wait_ge(turned_ready, b + 1)
                        pe.sem_inc(xn_free, 1)
                ins.then_inc(logits_ready, 1)
                pe.wait_ge(loaded, 16 * (len(plain) - 1))
                for k in range(1, len(squares)):
                    turn_square(k)
                if capped:
                    pe.wait_ge(constants, 2 * E + 1)
                    pe.wait_ge(counts_ready, 1)
                    pe.matmul(total[:, :], ones[:, :], counts[:, :], start=True, stop=True).then_inc(total_ready, 1)

            @block.scalar
            def _(act):
                def keep_square(k):
                    _, dst, at, r = squares[k]
                    act.wait_ge(square_ready, k + 1)
                    act.copy(dst[:, at, 0:r], ring[k % len(ring)][:, 0:r]).then_inc(square_free, 1)

                act.sem_inc(turned_free, 2)
                act.wait_ge(var_ready, 1)
                act.activation(std[:, :], var[:, :], ACT.Sqrt).then_inc(std_ready, 1)
                keep_square(0)
                with act.Fori(0, BLKS // 2) as i:
                    for slot in range(2):
                        act.wait_ge(turned_ready, i * 2 + slot + 1)
                        act.copy(xT[:, ds((i * 2 + slot) * BLK, BLK)], turned[slot][:, :]).then_inc(turned_free, 1)
                act.wait_ge(shifted, 1)
                act.activation(p[:, :, :], tmp[:, :, :], ACT.Exp).then_inc(exp_ready, 1)
                for k in range(1, len(squares)):
                    keep_square(k)


def experts(nc, x, xT, gates, w1T, w2T):
    units = E + 2
    pairs = E + 1
    HR, YR = 5, 3
    adds = E * TPB + 1

    def added(k):
        return (k + 1) * TPB if k < E else adds

    with Scope(nc) as sc:
        hidden = [sc.ps(f"hidden{i}", [P, BLK]) for i in range(HR)]
        y = [sc.ps(f"y{i}", [P, TPB, P]) for i in range(YR)]
        relu = sc.sb("relu", [P, 2, BLK])
        act_h = sc.sb("act_h", [P, HR, BLK])
        hidden_ready, hidden_free, relu_ready, relu_free = (
            sc.sem(n) for n in ("hidden_ready", "hidden_free", "relu_ready", "relu_free"))
        act_ready, y_ready, x_added = (sc.sem(n) for n in ("act_ready", "y_ready", "x_added"))

        with nc.Block() as block:
            @block.tensor
            def _(pe):
                pe.sem_inc(y_ready, pairs)
                with pe.Fori(0, BLKS) as i:
                    def second(k):
                        us = [k] if k < E else list(range(E, units))
                        pe.wait_ge(act_ready, i * units + us[-1] + 1)
                        pe.wait_ge(x_added, i * adds + added((k - YR) % pairs) + (adds if k >= YR else 0))
                        for t in range(TPB):
                            for u in us:
                                ins = pe.matmul(y[k % YR][:, t, :], act_h[:, u % HR, t * P:(t + 1) * P],
                                                w2T[:, u, :], start=(u == us[0]), stop=(u == us[-1]))
                        ins.then_inc(y_ready, 1)

                    for u in range(units):
                        pe.wait_ge(hidden_free, i * units + u + 1)
                        pe.matmul(hidden[u % HR][:, :], w1T[:, u, :], xT[:, ds(i * BLK, BLK)],
                                  start=True, stop=True).then_inc(hidden_ready, 1)
                        if 2 <= u < E + 2:
                            second(u - 2)
                    for k in range(units - 2, pairs):
                        second(k)

            @block.scalar
            def _(act):
                act.sem_inc(hidden_free, HR)
                with act.Fori(0, BLKS) as i:
                    for u in range(units):
                        act.wait_ge(hidden_ready, i * units + u + 1)
                        act.wait_ge(relu_free, i * units + u + 1)
                        act.activation(relu[:, u % 2, :], hidden[u % HR][:, :], ACT.Relu).then_inc(relu_ready, 1)
                        act.wait_ge(relu_ready, i * units + u + 1)
                        act.sem_inc(hidden_free, 1)

            @block.gpsimd
            def _(pool):
                pool.sem_inc(relu_free, 2)
                with pool.Fori(0, BLKS) as i:
                    for u in range(units):
                        pool.wait_ge(relu_ready, i * units + u + 1)
                        k = min((u - HR) % units, pairs - 1)
                        pool.wait_ge(y_ready, i * pairs + k + 1 + (pairs if u >= HR else 0))
                        r = relu[:, u % 2, :]
                        pool.tensor_tensor(act_h[:, u % HR, :], r, r, ALU.mult).then_inc(act_ready, 1)
                        pool.wait_ge(act_ready, i * units + u + 1)
                        pool.sem_inc(relu_free, 1)

            @block.vector
            def _(v):
                v.sem_inc(x_added, adds)
                with v.Fori(0, BLKS) as i:
                    for k in range(pairs):
                        v.wait_ge(y_ready, i * pairs + pairs + k + 1)
                        if k == E:
                            v.wait_ge(x_added, i * adds + adds + added(k - 1))
                            part = x[:, ds(i * TPB, TPB), :]
                            v.scalar_tensor_tensor(out=part, in0=y[k % YR][:, :, :], scalar=0.5, in1=part,
                                                   op0=ALU.mult, op1=ALU.add).then_inc(x_added, 1)
                            continue
                        for t in range(TPB):
                            if k:
                                v.wait_ge(x_added, i * adds + adds + added(k - 1) - (TPB - 1 - t))
                            part = x[:, ds(i * TPB + t, 1), :].rearrange("p a c -> p (a c)")
                            gate = gates[:, ds(i * TPB + t, 1), k:k + 1].rearrange("p a e -> p (a e)")
                            v.scalar_tensor_tensor(out=part, in0=y[k % YR][:, t, :], scalar=gate, in1=part,
                                                   op0=ALU.mult, op1=ALU.add).then_inc(x_added, 1)


def kept_experts(nc, x, xT, gates, kept, w1T, b1T, w2T, b2):
    with Scope(nc) as sc:
        w1_e, b1_e = sc.sb("w1_e", [P, P]), sc.sb("b1_e", [P, 1])
        b2_row, one_row = sc.sb("b2_row", [P, E * P]), sc.sb("one_row", [P, P])
        hidden = [sc.ps(f"hidden{i}", [P, BLK]) for i in range(2)]
        y = [sc.ps(f"y{i}", [P, TPB, P]) for i in range(2)]
        act_h = sc.sb("act_h", [P, 2, BLK])
        b2_loaded, zeroed, one_ready, staged, hidden_ready, act_ready, y_ready, x_added, passed = (sc.sem(n) for n in (
            "b2_loaded", "zeroed", "one_ready", "staged", "hidden_ready", "act_ready", "y_ready", "x_added", "passed"))

        @contextmanager
        def each(eng):
            with eng.Fori(0, E) as j:
                with eng.If(eng.value_load(kept[:, 0, ds(j, 1)], min_val=0, max_val=1) > 0):
                    yield j, eng.value_load(kept[:, 1, ds(j, 1)], min_val=0, max_val=E - 1)
                    eng.nop()
                eng.nop()

        with nc.Block() as block:
            @block.sync
            def _(sp):
                sp.wait_ge(zeroed, 2)
                sp.dma_start(b2_row[0:1, :], b2.rearrange("(a e) c -> a (e c)", a=1)).then_inc(b2_loaded, 16)

            @block.gpsimd
            def _(pool):
                for rows in (b2_row, one_row):
                    pool.memset(rows[:, :], 0.0).then_inc(zeroed, 1)
                pool.wait_ge(zeroed, 2)
                pool.memset(one_row[0:1, :], 1.0).then_inc(one_ready, 1)
                with each(pool) as (j, e):
                    wait_apart(pool, hidden_ready, j * BLKS + BLKS, passed)
                    wait_apart(pool, act_ready, j * BLKS + BLKS, passed)
                    pool.tensor_copy(w1_e[:, :], w1T[:, ds(e, 1), :].rearrange("p a f -> p (a f)")).then_inc(staged, 1)
                    pool.tensor_copy(b1_e[:, :], b1T[:, ds(e, 1)]).then_inc(staged, 1)

            @block.tensor
            def _(pe):
                pe.sem_inc(hidden_ready, BLKS)
                pe.sem_inc(y_ready, 2)
                pe.wait_ge(b2_loaded, 16)
                pe.wait_ge(one_ready, 1)
                with each(pe) as (j, e):
                    wait_apart(pe, staged, j * 2 + 2, passed)
                    with pe.Fori(0, BLKS // 2) as i:
                        for s in range(2):
                            wait_apart(pe, act_ready, j * BLKS + i * 2 + s + BLKS - 1, passed)
                            pe.matmul(hidden[s][:, :], w1_e[:, :], xT[:, ds((i * 2 + s) * BLK, BLK)],
                                      start=True, stop=True).then_inc(hidden_ready, 1)
                        for s in range(2):
                            wait_apart(pe, act_ready, j * BLKS + i * 2 + s + BLKS + 1, passed)
                            wait_apart(pe, x_added, (j * BLKS + i * 2 + s) * TPB + TILES - TPB, passed)
                            for t in range(TPB):
                                pe.matmul(y[s][:, t, :], one_row[:, :], b2_row[:, ds(e * P, P)],
                                          start=True, stop=False)
                                ins = pe.matmul(y[s][:, t, :], act_h[:, s, t * P:(t + 1) * P],
                                                w2T[:, ds(e, 1), :].rearrange("p a c -> p (a c)"),
                                                start=False, stop=True)
                            ins.then_inc(y_ready, 1)
                    pe.nop()

            @block.scalar
            def _(act):
                act.sem_inc(act_ready, BLKS)
                with each(act) as (j, e):
                    wait_apart(act, staged, j * 2 + 2, passed)
                    for i in range(BLKS):
                        act.wait_ge(hidden_ready, j * BLKS + i + BLKS + 1)
                        act.wait_ge(y_ready, j * BLKS + i + 1)
                        act.activation(act_h[:, i % 2, :], hidden[i % 2][:, :], ACT.Silu,
                                       bias=b1_e[:, :]).then_inc(act_ready, 1)

            @block.vector
            def _(v):
                v.sem_inc(x_added, TILES)
                with each(v) as (j, e):
                    with v.Fori(0, BLKS // 2) as i:
                        for s in range(2):
                            wait_apart(v, y_ready, j * BLKS + i * 2 + s + 3, passed)
                            wait_apart(v, x_added, (j * BLKS + i * 2 + s) * TPB + TPB, passed)
                            for t in range(TPB):
                                tile = (i * 2 + s) * TPB + t
                                part = x[:, ds(tile, 1), :].rearrange("p a c -> p (a c)")
                                gate = gates[:, ds(tile, 1), ds(e, 1)].rearrange("p a e -> p (a e)")
                                v.scalar_tensor_tensor(out=part, in0=y[s][:, t, :], scalar=gate, in1=part,
                                                       op0=ALU.mult, op1=ALU.add).then_inc(x_added, 1)
                    v.nop()


def ffn0(nc, x, ident, router, w1, w2, ws1, ws2):
    with Scope(nc) as sc:
        xT, gates = sc.sb("xT", [P, TILES * P]), sc.sb("gates", [P, TILES, E])
        w1T, w2T, routerT = sc.sb("w1T", [P, E + 2, P]), sc.sb("w2T", [P, E + 2, P]), sc.sb("routerT", [P, 1, P])
        normalise_and_route(nc, x, ident, xT, [
            (router, routerT[:, :, :]), (w1.rearrange("e f c -> (e f) c"), w1T[:, 0:E, :]), (ws1, w1T[:, E:E + 2, :]),
            (w2.rearrange("e d f -> (e d) f"), w2T[:, 0:E, :]), (ws2, w2T[:, E:E + 2, :])], routerT, gates)
        experts(nc, x, xT, gates, w1T, w2T)


def ffn1(nc, x, ident, gate_w, w1, b1, w2, b2):
    with Scope(nc) as sc:
        xT, gates = sc.sb("xT", [P, TILES * P]), sc.sb("gates", [P, TILES, E])
        w1T, w2T, routerT = sc.sb("w1T", [P, E, P]), sc.sb("w2T", [P, E, P]), sc.sb("routerT", [P, 1, P])
        b1T, kept = sc.sb("b1T", [P, 1, P]), sc.sb("kept", [1, 2, E], I32)
        normalise_and_route(nc, x, ident, xT, [
            (gate_w, routerT[:, :, :]), (w1.rearrange("e f c -> (e f) c"), w1T[:, :, :]), (b1, b1T[:, :, :]),
            (w2.rearrange("e d f -> (e d) f"), w2T[:, :, :])], routerT, gates, kept)
        kept_experts(nc, x, xT, gates, kept, w1T, b1T[:, 0, :], w2T, b2)


def s6(nc, x, ident, W_in, W_conv, W_x, W_dt, b_dt, A_log, D_param, W_out):
    T = TILES * P
    with Scope(nc) as sc:
        raw = sc.sb("raw", [P, DI, BATCHES, SEQ + 2])
        gate = sc.sb("gate", [P, DI, BATCHES, SEQ])
        u = sc.sb("u", [P, DI, BATCHES, SEQ])
        bc = sc.sb("bc", [3 * 2 * NS, T], BF16)
        delta = sc.sb("delta", [P, DI, BATCHES, SEQ])
        conv_w, a_neg = sc.sb("conv_w", [P, DI, 3]), sc.sb("a_neg", [P, DI, NS])
        wx, wdt = sc.sb("wx", [P, DI, DR + 2 * NS]), sc.sb("wdt", [DR, DI * P])
        wout = sc.sb("wout", [P, DI, P])
        bdt, dparam = sc.sb("bdt", [P, DI]), sc.sb("dparam", [P, DI])
        with Scope(nc) as front:
            dt = front.sb("dt", [DR, T])
            with Scope(nc) as inner:
                xT, win = inner.sb("xT", [P, T]), inner.sb("win", [P, 2 * DI * P])
                normalise(nc, x, ident, xT)
                s6_inner(nc, xT, win, W_in, W_conv, W_x, W_dt, b_dt, A_log, D_param, W_out, raw, gate, u, bc, dt,
                         conv_w, a_neg, wx, wdt, wout, bdt, dparam)
            s6_delta(nc, dt, wdt, bdt, u, delta, raw)
        s6_scan(nc, x, ident, bc, delta, raw, u, gate, a_neg, dparam, wout)


def s6_inner(nc, xT, win, W_in, W_conv, W_x, W_dt, b_dt, A_log, D_param, W_out, raw, gate, u, bc, dt, conv_w, a_neg,
             wx, wdt, wout, bdt, dparam):
    HB = SEQ // BLK
    with Scope(nc) as sc:
        conv = sc.sb("conv", [P, 2, SEQ])
        inner = [[sc.ps(f"inner{s}_{m}", [P, BLK]) for m in range(2 * DI)] for s in range(2)]
        loaded, zeroed, dve_done = sc.sem("loaded"), sc.sem("zeroed"), sc.sem("dve_done")
        inner_ready, inner_free, raw_ready, conv_ready, conv_free, u_ready, xd_ready, xd_free = (
            sc.sem(n) for n in ("inner_ready", "inner_free", "raw_ready", "conv_ready", "conv_free", "u_ready",
                                "xd_ready", "xd_free"))
        rest, mid = sc.sb("rest", [2 * NS, 2, BLK]), sc.sb("mid", [2 * NS, 2, BLK], BF16)
        act_done, dt_copied, bc_split, passed = (sc.sem(n) for n in ("act_done", "dt_copied", "bc_split", "passed"))
        loads = [(win[:, :], W_in), (conv_w[:, :, :], W_conv.rearrange("(h p) k -> p h k", p=P)),
                 (wx[:, :, :], W_x.rearrange("(h p) k -> p h k", p=P)), (wdt[:, :], W_dt),
                 (a_neg[:, :, :], A_log.rearrange("(h p) n -> p h n", p=P)),
                 (wout[:, :, :], W_out.rearrange("(h p) c -> p h c", p=P)),
                 (bdt[:, :], b_dt.rearrange("(h p) -> p h", p=P)),
                 (dparam[:, :], D_param.rearrange("(h p) -> p h", p=P))]
        with nc.Block() as block:
            @block.sync
            def _(sp):
                for dst, src in loads:
                    sp.dma_start(dst, src, allow_slow_non_contiguous=True).then_inc(loaded, 16)

            @block.tensor
            def _(pe):
                pe.wait_ge(loaded, 16 * len(loads))
                pe.sem_inc(inner_free, 2)
                with pe.Fori(0, BATCHES) as b:
                    for s in range(HB):
                        pe.wait_ge(inner_free, b * HB + s + 1)
                        for m in range(2 * DI):
                            ins = pe.matmul(inner[s][m][:, :], win[:, m * P:(m + 1) * P],
                                            xT[:, ds(b * SEQ + s * BLK, BLK)], start=True, stop=True)
                        ins.then_inc(inner_ready, 1)
                pe.wait_ge(inner_free, BATCHES * HB + 2)
                pe.sem_inc(xd_free, 4)
                with pe.Fori(0, BATCHES) as b:
                    wait_apart(pe, u_ready, b * DI + DI, passed)
                    for s in range(HB):
                        pe.wait_ge(xd_free, (b * HB + s + 1) * 2)
                        for rows, first, last in ((DR, 0, DR), (2 * NS, DR, DR + 2 * NS)):
                            for h in range(DI):
                                ins = pe.matmul(inner[s][first // DR][0:rows, :], wx[:, h, first:last],
                                                u[:, h, ds(b, 1), s * BLK:(s + 1) * BLK]
                                                .rearrange("p a l -> p (a l)"), start=(h == 0), stop=(h == DI - 1))
                        ins.then_inc(xd_ready, 1)

            @block.scalar
            def _(act):
                ch = Chain(act, act_done)
                act.wait_ge(loaded, 16 * len(loads))
                ch.link(act.activation(a_neg[:, :, :], a_neg[:, :, :], ACT.Exp))
                ch.inc(act.activation(a_neg[:, :, :], a_neg[:, :, :], ACT.Copy, scale=-1.0))
                act.wait_ge(zeroed, 1)

                def halves(b):
                    for s in range(HB):
                        act.wait_ge(inner_ready, b * HB + s + 1)
                        for h in range(DI):
                            ins = act.copy(raw[:, h, ds(b, 1), 2 + s * BLK:2 + (s + 1) * BLK]
                                           .rearrange("p a l -> p (a l)"), inner[s][h][:, :])
                        ins.then_inc(raw_ready, 1)
                        for h in range(DI):
                            last = ch.inc(act.activation(gate[:, h, ds(b, 1), s * BLK:(s + 1) * BLK]
                                                         .rearrange("p a l -> p (a l)"), inner[s][DI + h][:, :],
                                                         ACT.Silu))
                        ch.wait(last)
                        act.sem_inc(inner_free, 1)

                def convolved(b):
                    for h in range(DI):
                        act.wait_ge(conv_ready, b * DI + h + 1)
                        act.activation(u[:, h, ds(b, 1), :].rearrange("p a l -> p (a l)"), conv[:, h, :],
                                       ACT.Silu).then_inc(u_ready, 1)

                halves(0)
                with ch.loop(BATCHES - 1, HB * DI) as b:
                    halves(b + 1)
                    convolved(b)
                convolved(BATCHES - 1)
                with act.Fori(0, BATCHES) as b:
                    for s in range(HB):
                        act.wait_ge(xd_ready, b * HB + s + 1)
                        act.copy(dt[:, ds(b * SEQ + s * BLK, BLK)], inner[s][0][0:DR, :]).then_inc(dt_copied, 1)
                        act.wait_ge(bc_split, b * HB + s + 1)
                        act.wait_ge(dt_copied, b * HB + s + 1)
                        act.sem_inc(xd_free, 2)

            @block.vector
            def _(v):
                ch = Chain(v, dve_done)
                v.memset(raw[:, :, :, 0:2], 0.0).then_inc(zeroed, 1)
                v.wait_ge(zeroed, 1)
                with ch.loop(BATCHES, 2 * DI) as b:
                    v.wait_ge(raw_ready, b * HB + HB)
                    v.wait_ge(conv_free, b * DI + 1)
                    for k in range(3):
                        for h in range(DI):
                            tap = raw[:, h, ds(b, 1), k:k + SEQ].rearrange("p a l -> p (a l)")
                            w = conv_w[:, h, k:k + 1]
                            if k == 0:
                                ch.inc(v.tensor_scalar(conv[:, h, :], tap, w, None, ALU.mult))
                                continue
                            ch.wait(ch.at + ch.n - 1 if k == 1 else ch.at + 2 * DI - 1 + h)
                            ins = v.scalar_tensor_tensor(out=conv[:, h, :], in0=tap, scalar=w, in1=conv[:, h, :],
                                                         op0=ALU.mult, op1=ALU.add)
                            if k == 1:
                                ch.inc(ins)
                            else:
                                ins.then_inc(conv_ready, 1)

                with ch.loop(BATCHES, HB * 4) as b:
                    for s in range(HB):
                        v.wait_ge(xd_ready, b * HB + s + 1)
                        at, src = ds(b * SEQ + s * BLK, BLK), inner[s][1][0:2 * NS, :]
                        ch.link(v.tensor_copy(bc[0:2 * NS, at], src))
                        ch.link(v.tensor_tensor(rest[:, s, :], src, bc[0:2 * NS, at], ALU.subtract))
                        ch.link(v.tensor_copy(mid[:, s, :], rest[:, s, :]))
                        ch.inc(v.tensor_copy(bc[2 * NS:4 * NS, at], mid[:, s, :]))
                        v.tensor_tensor(bc[4 * NS:6 * NS, at], rest[:, s, :], mid[:, s, :],
                                        ALU.subtract).then_inc(bc_split, 1)

            @block.gpsimd
            def _(pool):
                pool.sem_inc(conv_free, 1)
                with pool.Fori(0, BATCHES) as b:
                    pool.wait_ge(u_ready, b * DI + DI)
                    pool.sem_inc(conv_free, DI)


def s6_delta(nc, dt, wdt, bdt, u, delta, du):
    HB = SEQ // BLK
    steps = BATCHES * DI
    with Scope(nc) as sc:
        z_ps = [sc.ps(f"z{i}", [P, SEQ]) for i in range(DI)]
        z, ex, w, ln = (sc.sb(n, [P, DI, SEQ]) for n in ("z", "ex", "w", "ln"))
        z_mm, z_free, z_ready, ex_ready, w_ready, ln_ready, step_done, dve_done, act_done = (
            sc.sem(n) for n in ("z_mm", "z_free", "z_ready", "ex_ready", "w_ready", "ln_ready", "step_done",
                                "dve_done", "act_done"))
        passed = sc.sem("passed")
        with nc.Block() as block:
            @block.tensor
            def _(pe):
                pe.sem_inc(z_free, DI)
                with pe.Fori(0, BATCHES) as b:
                    for h in range(DI):
                        wait_apart(pe, z_free, b * DI + h + 1, passed)
                        for s in range(HB):
                            ins = pe.matmul(z_ps[h][:, s * BLK:(s + 1) * BLK], wdt[:, h * P:(h + 1) * P],
                                            dt[:, ds(b * SEQ + s * BLK, BLK)], start=True, stop=True)
                        ins.then_inc(z_mm, 1)

            @block.scalar
            def _(act):
                ch = Chain(act, act_done)
                act.sem_inc(step_done, DI)
                with ch.loop(BATCHES, DI) as b:
                    for h in range(DI):
                        act.wait_ge(z_mm, b * DI + h + 1)
                        act.wait_ge(step_done, b * DI + h + 1)
                        act.activation(z[:, h, :], z_ps[h][:, :], ACT.Identity,
                                       bias=bdt[:, h:h + 1]).then_inc(z_ready, 1)
                        act.wait_ge(z_ready, b * DI + h + 1)
                        act.sem_inc(z_free, 1)
                        ch.link(act.activation(ex[:, h, :], z[:, h, :], ACT.Abs))
                        act.activation(ex[:, h, :], ex[:, h, :], ACT.Exp, scale=-1.0).then_inc(ex_ready, 1)
                    for h in range(DI):
                        act.wait_ge(w_ready, b * DI + h + 1)
                        act.activation(ln[:, h, :], w[:, h, :], ACT.Ln).then_inc(ln_ready, 1)

            @block.vector
            def _(v):
                ch = Chain(v, dve_done)
                with ch.loop(BATCHES, 3 * DI) as b:
                    for h in range(DI):
                        v.wait_ge(ex_ready, b * DI + h + 1)
                        v.wait_ge(step_done, b * DI + h + 1)
                        v.tensor_scalar(w[:, h, :], ex[:, h, :], 1.0, None, ALU.add).then_inc(w_ready, 1)
                        v.wait_ge(w_ready, b * DI + h + 1)
                        ch.inc(v.scalar_tensor_tensor(out=ex[:, h, :], in0=w[:, h, :], scalar=-1.0, in1=ex[:, h, :],
                                                      op0=ALU.add, op1=ALU.subtract))
                    for h in range(DI):
                        v.wait_ge(ln_ready, b * DI + h + 1)
                        ch.link(v.tensor_tensor(ln[:, h, :], ln[:, h, :], ex[:, h, :], ALU.subtract))
                        d = delta[:, h, ds(b, 1), :].rearrange("p a l -> p (a l)")
                        ch.link(v.scalar_tensor_tensor(out=d, in0=z[:, h, :], scalar=0.0, in1=ln[:, h, :],
                                                       op0=ALU.max, op1=ALU.add))
                        v.tensor_tensor(du[:, h, ds(b, 1), 0:SEQ].rearrange("p a l -> p (a l)"), d,
                                        u[:, h, ds(b, 1), :].rearrange("p a l -> p (a l)"),
                                        ALU.mult).then_inc(step_done, 1)


def s6_scan(nc, x, ident, bc, delta, du, u, gate, a_neg, dparam, wout):
    HB = SEQ // BLK
    G = NS * DI
    R, RH = 2, 4
    with Scope(nc) as sc:
        dA, dBu = sc.sb("dA", [P, R, SEQ]), sc.sb("dBu", [P, R, SEQ])
        hs = sc.sb("hs", [P, RH, SEQ])
        sel = sc.sb("sel", [3 * 2 * NS, 2 * NS], BF16)
        b_sb = sc.sb("b_sb", [P, 2, SEQ])
        yg = sc.sb("yg", [P, DI, SEQ])
        b_ps, c_ps = sc.ps("b_ps", [P, SEQ]), sc.ps("c_ps", [P, SEQ])
        y_ps = [sc.ps(f"y_ps{h}", [P, SEQ]) for h in range(DI)]
        sel_step, passed = sc.sem("sel_step"), sc.sem("passed")
        names = ("b_ready", "b_copied", "c_ready", "dA_ready", "dBu_ready", "h_ready",
                 "hC_ready", "y_summed", "y_done", "skip_added", "yg_ready", "out_ready", "x_added")
        (b_ready, b_copied, c_ready, dA_ready, dBu_ready, h_ready, hC_ready, y_summed, y_done,
         skip_added, yg_ready, out_ready, x_added) = (sc.sem(n) for n in names)

        def slot(g):
            return g % R

        def row(t, h, b):
            return t[:, h, ds(b, 1), 0:SEQ].rearrange("p a l -> p (a l)")

        with nc.Block() as block:
            @block.gpsimd
            def _(pool):
                pool.memset(sel[:, :], 0.0).then_inc(sel_step, 1)
                for k in range(3):
                    pool.wait_ge(sel_step, k + 1)
                    pool.affine_select(out=sel[:, :], in_=sel[:, :], compare_op=ALU.not_equal, fill=1.0,
                                       base=-2 * NS * k, pattern=[[-1, 2 * NS]], channel_multiplier=1)\
                        .then_inc(sel_step, 1)
                with pool.Fori(0, BATCHES) as b:
                    for g in range(G):
                        n, h = g // DI, g % DI
                        pool.wait_ge(b_copied, b * NS + n + 1)
                        wait_apart(pool, h_ready, b * G + g - R + 1 + G, passed)
                        pool.tensor_tensor(dBu[:, slot(g), :], row(du, h, b), b_sb[:, n % 2, :],
                                           ALU.mult).then_inc(dBu_ready, 1)

            @block.scalar
            def _(act):
                with act.Fori(0, BATCHES) as b:
                    for g in range(G):
                        n, h = g // DI, g % DI
                        if h == 0:
                            act.wait_ge(b_ready, b * NS + n + 1)
                            if n >= 2:
                                act.wait_ge(dBu_ready, b * G + (n - 1) * DI)
                            act.copy(b_sb[:, n % 2, :], b_ps[:, :]).then_inc(b_copied, 1)
                        wait_apart(act, h_ready, b * G + g - R + 1 + G, passed)
                        act.activation(dA[:, slot(g), :], row(delta, h, b), ACT.Exp,
                                       scale=a_neg[:, h, n:n + 1]).then_inc(dA_ready, 1)

            @block.vector
            def _(v):
                v.sem_inc(h_ready, G)
                with v.Fori(0, BATCHES) as b:
                    def scan(g):
                        v.wait_ge(dA_ready, b * G + g + 1)
                        v.wait_ge(dBu_ready, b * G + g + 1)
                        v.wait_ge(y_summed, b * G + g - RH + 1 + G)
                        v.tensor_tensor_scan(hs[:, g % RH, :], dA[:, slot(g), :], dBu[:, slot(g), :], 0.0,
                                             ALU.mult, ALU.add).then_inc(h_ready, 1)

                    def times_c(g):
                        v.wait_ge(h_ready, b * G + G + g + 1)
                        v.wait_ge(c_ready, b * NS + g // DI + 1)
                        v.tensor_tensor(hs[:, g % RH, :], hs[:, g % RH, :], c_ps[:, :],
                                        ALU.mult).then_inc(hC_ready, 1)

                    scan(0)
                    for g in range(1, G + 1):
                        if g < G:
                            scan(g)
                        times_c(g - 1)
                    v.wait_ge(y_done, b + 1)
                    v.wait_ge(out_ready, b * HB + HB)
                    for s in range(HB):
                        at = slice(s * BLK, (s + 1) * BLK)
                        for h in range(DI):
                            v.scalar_tensor_tensor(out=yg[:, h, at], in0=row(u, h, b)[:, at],
                                                   scalar=dparam[:, h:h + 1], in1=y_ps[h][:, at], op0=ALU.mult,
                                                   op1=ALU.add).then_inc(skip_added, 1)
                        for h in range(DI):
                            v.wait_ge(skip_added, (b * HB + s) * DI + h + 1)
                            v.tensor_tensor(yg[:, h, at], yg[:, h, at], row(gate, h, b)[:, at],
                                            ALU.mult).then_inc(yg_ready, 1)
                    for s in range(HB):
                        v.wait_ge(out_ready, b * HB + s + 1 + HB)
                        part = x[:, ds(b * BT + s * TPB, TPB), :].rearrange("p t c -> p (t c)")
                        v.tensor_tensor(part, part, y_ps[0][:, s * BLK:(s + 1) * BLK], ALU.add).then_inc(x_added, 1)

            @block.tensor
            def _(pe):
                pe.wait_ge(sel_step, 4)
                pe.sem_inc(y_summed, G)
                pe.sem_inc(out_ready, HB)
                pe.sem_inc(x_added, HB)

                def spread(dst, m, b, ready):
                    for s in range(HB):
                        ins = pe.matmul(dst[:, s * BLK:(s + 1) * BLK],
                                        sel[:, m:m + 1].to_broadcast([3 * 2 * NS, P]),
                                        bc[:, ds(b * SEQ + s * BLK, BLK)], start=True, stop=True)
                    ins.then_inc(ready, 1)

                spread(b_ps, 0, 0, b_ready)
                with pe.Fori(0, BATCHES) as b:
                    def spread_b(n):
                        wait_apart(pe, b_copied, b * NS + n, passed)
                        spread(b_ps, n, b, b_ready)

                    def sum_y(g):
                        n, h = g // DI, g % DI
                        pe.wait_ge(hC_ready, b * G + g + 1)
                        for s in range(HB):
                            ins = pe.matmul(y_ps[h][:, s * BLK:(s + 1) * BLK], ident[:, :],
                                            hs[:, g % RH, s * BLK:(s + 1) * BLK], start=(n == 0), stop=(n == NS - 1),
                                            skip_group_check=True)
                        ins.then_inc(y_summed, 1)

                    for n in range(NS):
                        if n == 1:
                            pe.wait_ge(x_added, b * HB + HB)
                        if n:
                            sum_y((n - 1) * DI)
                            pe.wait_ge(hC_ready, b * G + n * DI)
                        spread(c_ps, NS + n, b, c_ready)
                        if n == 0:
                            spread_b(1)
                        if n:
                            sum_y((n - 1) * DI + 1)
                        if n + 2 < NS:
                            spread_b(n + 2)
                    sum_y(G - 2)
                    sum_y(G - 1)
                    pe.wait_ge(y_summed, b * G + 2 * G)
                    pe.sem_inc(y_done, 1)
                    wait_apart(pe, b_copied, b * NS + NS, passed)
                    spread(b_ps, 0, (b + 1) % BATCHES, b_ready)
                    for s in range(HB):
                        pe.wait_ge(yg_ready, (b * HB + s + 1) * DI)
                        for t in range(s * TPB, (s + 1) * TPB):
                            for h in range(DI):
                                ins = pe.matmul(y_ps[0][:, t * P:(t + 1) * P], yg[:, h, t * P:(t + 1) * P],
                                                wout[:, h, :], start=(h == 0), stop=(h == DI - 1))
                        ins.then_inc(out_ready, 1)


def attention(nc, x, ident, Wq, bq, Wk, bk, Wv, bv, Wo, bo, phase, interference):
    with Scope(nc) as sc:
        xT = sc.sb("xT", [P, TILES * P])
        V = sc.sb("V", [P, TILES, P])
        wq, wk, wo = (sc.sb(n, [P, P]) for n in ("wq", "wk", "wo"))
        bqh, bkh = sc.sb("bqh", [1 + D, H]), sc.sb("bkh", [1 + D, H])
        scale_w, share_w = sc.sb("scale_w", [P, WL * H]), sc.sb("share_w", [P, WL])
        bq_col, bk_col, cos_is_one = sc.sb("bq_col", [P, 1]), sc.sb("bk_col", [P, 1]), sc.sb("cos_is_one", [1, 1], I32)
        normalise(nc, x, ident, xT)
        att_setup(nc, x, xT, V, wq, wk, wo, bqh, bkh, bq_col, bk_col, scale_w, share_w, Wq, bq, Wk, bk, Wv, bv, Wo, bo, phase,
                  interference)
        att_bound(nc, ident, xT, wq, wk, bq_col, bk_col, cos_is_one)
        att_heads(nc, ident, xT, V, wq, wk, bqh, bkh, scale_w, share_w, cos_is_one)
        att_heads_cosine(nc, ident, xT, V, wq, wk, bqh, bkh, scale_w, share_w, cos_is_one)
        att_out(nc, x, ident, V, wo)


def att_setup(nc, x, xT, V, wq, wk, wo, bqh, bkh, bq_col, bk_col, scale_w, share_w, Wq, bq, Wk, bk, Wv, bv, Wo, bo, phase,
              interference):
    with Scope(nc) as sc:
        wv, bv_b, bo_b = (sc.sb(n, [P, P]) for n in ("wv", "bv_b", "bo_b"))
        turns, angle = sc.sb("turns", [P, WL * H]), sc.sb("angle", [P, WL * H])
        v_ps = [sc.ps(f"v_ps{i}", [P, TPB, P]) for i in range(2)]
        loaded, bias_zero, angle_ready, cos_ready, dve_done, v_mm, v_ready, x_ready, act_done = (
            sc.sem(n) for n in ("loaded", "bias_zero", "angle_ready", "cos_ready", "dve_done", "v_mm", "v_ready",
                                "x_ready", "act_done"))
        head_rows = "(h d) -> d h"
        loads = [(wv[:, :], Wv), (bv_b[:, :], bv.partition_broadcast(P)), (bo_b[:, :], bo.partition_broadcast(P)),
                 (scale_w[:, :], phase.rearrange("w h -> (w h)").partition_broadcast(P)),
                 (share_w[:, :], interference.partition_broadcast(P)), (wq[:, :], Wq), (wk[:, :], Wk),
                 (wo[:, :], Wo), (bqh[1:1 + D, :], bq.rearrange(head_rows, d=D)),
                 (bkh[1:1 + D, :], bk.rearrange(head_rows, d=D)), (bq_col[:, :], bq.rearrange("(p a) -> p a", a=1)),
                 (bk_col[:, :], bk.rearrange("(p a) -> p a", a=1))]
        with nc.Block() as block:
            @block.sync
            def _(sp):
                sp.wait_ge(bias_zero, 2)
                for dst, src in loads:
                    sp.dma_start(dst, src, allow_slow_non_contiguous=True).then_inc(loaded, 16)

            @block.tensor
            def _(pe):
                pe.wait_ge(loaded, 16 * len(loads))
                for i in range(BLKS):
                    if i >= 2:
                        pe.wait_ge(v_ready, i - 1)
                    for t in range(TPB):
                        ins = pe.matmul(v_ps[i % 2][:, t, :], xT[:, (i * TPB + t) * P:(i * TPB + t + 1) * P],
                                        wv[:, :], start=True, stop=True)
                    ins.then_inc(v_mm, 1)

            @block.gpsimd
            def _(pool):
                pool.wait_ge(loaded, 16 * len(loads))
                pool.tensor_tensor(x[:, :, :], x[:, :, :], bo_b[:, :].unsqueeze(1).to_broadcast([P, TILES, P]),
                                   ALU.add).then_inc(x_ready, 1)
                pool.wait_ge(x_ready, 1)

            @block.scalar
            def _(act):
                ch = Chain(act, act_done)
                act.wait_ge(angle_ready, 1)
                ch.link(act.activation(angle[:, :], angle[:, :], ACT.Sin))
                act.activation(scale_w[:, :], angle[:, :], ACT.Square).then_inc(cos_ready, 1)

            @block.vector
            def _(v):
                ch = Chain(v, dve_done)
                v.memset(bqh[:, :], 0.0).then_inc(bias_zero, 1)
                v.memset(bkh[:, :], 1.0).then_inc(bias_zero, 1)
                v.wait_ge(loaded, 16 * len(loads))
                ch.inc(v.tensor_scalar(share_w[:, :], share_w[:, :], 1.0 / WL, None, ALU.mult))
                ch.link(v.tensor_scalar(turns[:, :], scale_w[:, :], 1.0 / (2 * float(np.pi)), ROUND, ALU.mult, ALU.add))
                ch.link(v.tensor_scalar(turns[:, :], turns[:, :], ROUND, None, ALU.subtract))
                src = scale_w
                for part in (TWO_PI_A, TWO_PI_B, TWO_PI_C):
                    ch.link(v.scalar_tensor_tensor(out=angle[:, :], in0=turns[:, :], scalar=-part, in1=src[:, :],
                                                   op0=ALU.mult, op1=ALU.add))
                    src = angle
                ch.link(v.tensor_scalar(turns[:, :], angle[:, :], -1.0, None, ALU.mult))
                ch.link(v.tensor_tensor(angle[:, :], angle[:, :], turns[:, :], ALU.max))
                v.tensor_scalar(angle[:, :], angle[:, :], -1.0, HALF_PI, ALU.mult, ALU.add).then_inc(angle_ready, 1)
                v.wait_ge(cos_ready, 1)
                ch.inc(v.tensor_scalar(scale_w[:, :], scale_w[:, :], SCALE, None, ALU.mult))
                for i in range(BLKS):
                    v.wait_ge(v_mm, i + 1)
                    v.tensor_tensor(V[:, i * TPB:(i + 1) * TPB, :], v_ps[i % 2][:, :, :],
                                    bv_b[:, :].unsqueeze(1).to_broadcast([P, TPB, P]), ALU.add).then_inc(v_ready, 1)


def att_heads(nc, ident, xT, V, wq, wk, bqh, bkh, scale_w, share_w, cos_is_one):
    KT = SEQ // P
    STEPS = 2 + BT + 1 + KT
    USE_Q, USE_K, USE_S, USE_M, USE_T = 0, 1, 2, 2 + BT, 3 + BT
    M = 32
    PER_TURN = 7
    assert (HEADS - 1) % PER_TURN == 0
    slices = [[2], [3, 4], [5], [6, 7], [8], [9], [USE_M]] + [[USE_T + k] for k in range(KT)]
    assert [u for s in slices for u in s] == list(range(USE_S, STEPS)) and len(slices) == WL - 1
    with Scope(nc) as sc:
        wqh, wkh = sc.sb("wqh", [P, 1 + D]), sc.sb("wkh", [P, 1 + D])
        Q, K = sc.sb("Q", [P, SEQ]), sc.sb("K", [P, SEQ])
        neg_max = sc.sb("neg_max", [P, BT])
        shifted = sc.sb("shifted", [P, 2, KT * SEQ])
        weights = sc.sb("weights", [P, 2, KT, SEQ])
        v_one = sc.sb("v_one", [P, KT, M])
        sums = sc.sb("sums", [P, 2, 2 * P])
        factor = sc.sb("factor", [P, 2, 2, 4])
        shares = sc.sb("shares", [P, WL, BT, D])
        wide = [sc.ps(f"wide{i}", [P, SEQ]) for i in range(2)]
        pv = [sc.ps(f"pv{i}", [P, 512]) for i in range(2)]
        turned = [sc.ps(f"turned{i}", [P, 2, 2, P]) for i in range(2)]
        (w_staged, v_staged, wide_ready, wide_read, exp_ready, pv_ready, sums_ready, turned_ready, turned_read,
         dve_done, pool_done, passed) = (sc.sem(n) for n in (
             "w_staged", "v_staged", "wide_ready", "wide_read", "exp_ready", "pv_ready", "sums_ready",
             "turned_ready", "turned_read", "dve_done", "pool_done", "passed"))

        def slice_of(t, n):
            return t[:, ds(n // H * BT, BT), ds(n % H * D, D)]

        with nc.Block() as block:
            @block.gpsimd
            def _(pool):
                ch = Chain(pool, pool_done)
                for w in (wqh, wkh):
                    ch.inc(pool.memset(w[:, 0:1], 0.0))
                ch.link(pool.memset(v_one[:, :, :], 0.0))
                ch.link(pool.memset(v_one[:, :, D:D + 1], 1.0))

                def stage_w(m):
                    pool.tensor_copy(wqh[:, 1:1 + D], wq[:, ds(m % H * D, D)]).then_inc(w_staged, 1)
                    pool.tensor_copy(wkh[:, 1:1 + D], wk[:, ds(m % H * D, D)]).then_inc(w_staged, 1)

                def head(n, last):
                    wait_apart(pool, pv_ready, n * WL + 2, passed)
                    pool.tensor_copy(v_one[:, :, 0:D], slice_of(V, n)).then_inc(v_staged, 1)
                    if not last:
                        wait_apart(pool, wide_ready, n * STEPS + STEPS + USE_K + 1, passed)
                        stage_w(n + 2)

                with pool.If(pool.value_load(cos_is_one[:, :], min_val=0, max_val=1) > 0):
                    stage_w(0)
                    pool.wait_ge(wide_ready, USE_K + 1)
                    stage_w(1)
                    with pool.Fori(0, HEADS - 1) as n:
                        head(n, False)
                    head(HEADS - 1, True)

            @block.scalar
            def _(act):
                def head(n):
                    wait_apart(act, wide_read, n * STEPS + 2 * STEPS, passed)
                    for w in range(WL):
                        wait_apart(act, pv_ready, n * WL + w + 1, passed)
                        act.activation(weights[:, w % 2, :, :].rearrange("p k q -> p (k q)"),
                                       shifted[:, ds(n % 2, 1), :].rearrange("p a q -> p (a q)"), ACT.Exp,
                                       scale=scale_w[:, ds(n % H + w * H, 1)]).then_inc(exp_ready, 1)

                with act.If(act.value_load(cos_is_one[:, :], min_val=0, max_val=1) > 0):
                    with act.Fori(0, (HEADS - 1) // PER_TURN) as turn:
                        for k in range(PER_TURN):
                            head(turn * PER_TURN + k)
                    head(HEADS - 1)

            @block.tensor
            def _(pe):
                def prepare(m, use):
                    bank = wide[use % 2]
                    back = {0: 0, 1: -1}.get(use, use - 1)
                    pe.wait_ge(wide_read, m * STEPS + STEPS + back)
                    if use in (USE_Q, USE_K):
                        w, count = (wqh, 1) if use == USE_Q else (wkh, 2)
                        wait_apart(pe, w_staged, m * 2 + count, passed)
                        for s in range(2):
                            ins = pe.matmul(bank[0:1 + D, s * BLK:(s + 1) * BLK], w[:, :],
                                            xT[:, ds(m % HEADS // H * SEQ + s * BLK, BLK)], start=True, stop=True)
                    elif use < USE_M:
                        i = use - USE_S
                        if i == 0:
                            pe.wait_ge(wide_read, m * STEPS + STEPS + USE_K + 1)
                        for s in range(2):
                            ins = pe.matmul(bank[:, s * BLK:(s + 1) * BLK], Q[:, i * P:(i + 1) * P],
                                            K[:, s * BLK:(s + 1) * BLK], start=True, stop=True)
                    elif use == USE_M:
                        pe.wait_ge(wide_read, m * STEPS + STEPS + USE_M)
                        for i in range(BT):
                            ins = pe.matmul(bank[0:1, i * P:(i + 1) * P], neg_max[:, i:i + 1], ident[:, :],
                                            start=True, stop=True)
                    else:
                        k = use - USE_T
                        if k == 0:
                            pe.wait_ge(wide_read, m * STEPS + STEPS + USE_M + 1)
                        for s in range(2):
                            ins = pe.matmul(bank[:, s * BLK:(s + 1) * BLK], K[:, k * P:(k + 1) * P],
                                            Q[:, s * BLK:(s + 1) * BLK], start=True, stop=True)
                    ins.then_inc(wide_ready, 1)

                def slice_part(n, w, part):
                    m, uses = (n + 1, slices[w]) if w < WL - 1 else (n + 2, [USE_Q, USE_K])
                    for use in uses[part:part + 1]:
                        prepare(m, use)

                def turn(n, w):
                    pe.wait_ge(sums_ready, n * WL + w + 3)
                    if w % 2 == 0:
                        pe.wait_ge(turned_read, n * (WL // 2) + w // 2 + 1)
                    for c in range(2):
                        ins = pe.transpose(turned[w // 2 % 2][:, w % 2, c, :], sums[:, w % 2, c * P:(c + 1) * P],
                                           ident[:, :])
                    ins.then_inc(turned_ready, 1)

                def head(n, last):
                    for w in range(WL):
                        if w == 0:
                            pe.wait_ge(v_staged, n + 1)
                        pe.wait_ge(exp_ready, n * WL + w + 1)
                        pe.wait_ge(sums_ready, n * WL + w + 1)
                        for k in range(KT):
                            if k == KT // 2 and not last:
                                slice_part(n, w, 0)
                            for j in range(4):
                                quarter = weights[:, w % 2, k, :].rearrange("p (c j q) -> p c j q", c=2, j=4)
                                ins = pe.matmul(pv[w % 2][M * j:M * j + M, 0:2 * P], v_one[:, k, :],
                                                quarter[:, :, j, :], start=(k == 0), stop=(k == KT - 1))
                        ins.then_inc(pv_ready, 1)
                        if w:
                            turn(n, w - 1)
                        if not last:
                            slice_part(n, w, 1)
                    turn(n, WL - 1)

                with pe.If(pe.value_load(cos_is_one[:, :], min_val=0, max_val=1) > 0):
                    pe.sem_inc(pv_ready, 2)
                    pe.sem_inc(turned_ready, 2)
                    for m, use in [(0, u) for u in range(STEPS)] + [(1, USE_Q), (1, USE_K)]:
                        prepare(m, use)
                    with pe.Fori(0, HEADS - 1) as n:
                        head(n, False)
                    head(HEADS - 1, True)

            @block.vector
            def _(v):
                ch = Chain(v, dve_done)

                def prepare(m, use):
                    bank = wide[use % 2]
                    v.wait_ge(wide_ready, m * STEPS + use + 1)
                    if use in (USE_Q, USE_K):
                        dst, bias = (Q, bqh) if use == USE_Q else (K, bkh)
                        ins = v.tensor_scalar(dst[0:1 + D, :], bank[0:1 + D, :], bias[:, ds(m % H, 1)], None, ALU.add)
                    elif use < USE_M:
                        i = use - USE_S
                        ins = v.tensor_reduce(neg_max[:, i:i + 1], bank[:, :], AX.X, ALU.max, negate=True)
                    elif use == USE_M:
                        ins = v.tensor_copy(Q[0:1, :], bank[0:1, :])
                    else:
                        k = use - USE_T
                        ins = v.tensor_copy(shifted[:, ds(m % 2, 1), k * SEQ:(k + 1) * SEQ]
                                            .rearrange("p a q -> p (a q)"), bank[:, :])
                    ins.then_inc(wide_read, 1)

                def slice_part(n, w, part):
                    m, uses = (n + 1, slices[w]) if w < WL - 1 else (n + 2, [USE_Q, USE_K])
                    for use in uses[part:part + 1]:
                        prepare(m, use)

                def divide(n, pair):
                    v.wait_ge(turned_ready, n * WL + 2 * pair + 4)
                    t = turned[pair % 2][:, :, :, :].rearrange("p w c (j m) -> p (w c j) m", m=M)
                    f = factor[:, :, :, :].rearrange("p w c j -> p (w c j)")
                    ch.link(v.reciprocal(f, t[:, :, D]))
                    ch.link(v.tensor_tensor(factor[:, :, :, :].rearrange("p w c j -> p w (c j)"),
                                            factor[:, :, :, :].rearrange("p w c j -> p w (c j)"),
                                            share_w[:, 2 * pair:2 * pair + 2].unsqueeze(2).to_broadcast([P, 2, BT]),
                                            ALU.mult))
                    v.tensor_tensor(shares[:, 2 * pair:2 * pair + 2, :, :].rearrange("p w t d -> p (w t) d"),
                                    t[:, :, 0:D], f.unsqueeze(2).to_broadcast([P, 2 * BT, D]),
                                    ALU.mult).then_inc(turned_read, 1)

                def head(n, last):
                    for w in range(WL):
                        if not last:
                            slice_part(n, w, 0)
                        v.wait_ge(pv_ready, n * WL + w + 3)
                        v.wait_ge(turned_ready, n * WL + w + 1)
                        v.tensor_copy(sums[:, w % 2, :], pv[w % 2][:, 0:2 * P]).then_inc(sums_ready, 1)
                        if not last:
                            slice_part(n, w, 1)
                        if w % 2 == 0 and w:
                            divide(n, w // 2 - 1)
                    divide(n, WL // 2 - 1)
                    v.wait_ge(turned_read, n * (WL // 2) + WL // 2 + 2)
                    ch.link(v.tensor_reduce(slice_of(V, n), shares[:, :, :, :].rearrange("p w t d -> p t d w"),
                                            AX.X, ALU.add))

                with v.If(v.value_load(cos_is_one[:, :], min_val=0, max_val=1) > 0):
                    v.sem_inc(wide_read, STEPS)
                    v.sem_inc(sums_ready, 2)
                    v.sem_inc(turned_read, 2)
                    for rows in (Q, K):
                        ch.link(v.memset(rows[:, :], 0.0))
                    for m, use in [(0, u) for u in range(STEPS)] + [(1, USE_Q), (1, USE_K)]:
                        prepare(m, use)
                    with ch.loop(HEADS - 1, WL + 1) as n:
                        head(n, False)
                    head(HEADS - 1, True)


def att_bound(nc, ident, xT, wq, wk, bq_col, bk_col, cos_is_one):
    with Scope(nc) as sc:
        proj = [sc.ps(f"proj{i}", [P, BLK]) for i in range(2)]
        biased = sc.sb("biased", [P, 2, BLK])
        tops, top = sc.sb("tops", [P, 2, BLKS]), sc.sb("top", [P, 2])
        row, pair, bound = sc.ps("row", [1, 2, P]), sc.sb("pair", [1, 2]), sc.sb("bound", [1, 1])
        mm, biased_ready, top_taken, top_ready, row_ready, dve_done = (
            sc.sem(n) for n in ("mm", "biased_ready", "top_taken", "top_ready", "row_ready", "dve_done"))
        with nc.Block() as block:
            @block.tensor
            def _(pe):
                pe.sem_inc(biased_ready, 2)
                with pe.Fori(0, BLKS) as i:
                    for j, w in enumerate((wq, wk)):
                        pe.wait_ge(biased_ready, i * 2 + j + 1)
                        pe.matmul(proj[j][:, :], w[:, :], xT[:, ds(i * BLK, BLK)], start=True,
                                  stop=True).then_inc(mm, 1)
                pe.wait_ge(top_ready, 2)
                for j in range(2):
                    ins = pe.matmul(row[:, j, :], top[:, j:j + 1], ident[:, :], start=True, stop=True)
                ins.then_inc(row_ready, 1)

            @block.scalar
            def _(act):
                act.sem_inc(top_taken, 2)
                with act.Fori(0, BLKS) as i:
                    for j, bias in enumerate((bq_col, bk_col)):
                        act.wait_ge(mm, i * 2 + j + 1)
                        act.wait_ge(top_taken, i * 2 + j + 1)
                        act.activation(biased[:, j, :], proj[j][:, :], ACT.Identity,
                                       bias=bias[:, 0:1]).then_inc(biased_ready, 1)

            @block.vector
            def _(v):
                ch = Chain(v, dve_done)
                with v.Fori(0, BLKS) as i:
                    for j in range(2):
                        v.wait_ge(biased_ready, i * 2 + j + 3)
                        v.tensor_reduce(tops[:, j, ds(i, 1)], biased[:, j, :], AX.X, ALU.max,
                                        apply_absolute_value=True).then_inc(top_taken, 1)
                v.wait_ge(top_taken, 2 * BLKS + 2)
                for j in range(2):
                    v.tensor_reduce(top[:, j:j + 1], tops[:, j, :], AX.X, ALU.max).then_inc(top_ready, 1)
                v.wait_ge(row_ready, 1)
                ch.link(v.tensor_reduce(pair[:, :], row[:, :, :], AX.X, ALU.max))
                ch.link(v.tensor_tensor(bound[:, :], pair[:, 0:1], pair[:, 1:2], ALU.mult))
                ch.link(v.tensor_scalar(cos_is_one[:, :], bound[:, :], D * SCALE, S_EXACT, ALU.mult, ALU.is_lt))


def att_heads_cosine(nc, ident, xT, V, wq, wk, bqh, bkh, scale_w, share_w, cos_is_one):
    with Scope(nc) as sc:
        wqh, wkh, vh = sc.sb("wqh", [P, 1 + D]), sc.sb("wkh", [P, 1 + D]), sc.sb("vh", [P, BT, D])
        Q, K = sc.sb("Q", [1 + D, SEQ]), sc.sb("K", [1 + D, SEQ])
        qk, s, arg, turns, angle, cosine, ex, mix, mixT = (
            sc.sb(n, [P, SEQ]) for n in ("qk", "s", "arg", "turns", "angle", "cosine", "ex", "mix", "mixT"))
        neg_max, den = sc.sb("neg_max", [P, 1]), sc.sb("den", [P, 1])
        heads = sc.sb("heads", [P, BT, D])
        proj, s_ps, mixT_ps = (sc.ps(n, [P, SEQ]) for n in ("proj", "s_ps", "mixT_ps"))
        o_ps = sc.ps("o_ps", [P, D])
        (staged, proj_mm, qk_ready, s_mm, angle_ready, cos_ready, max_ready, exp_ready, mix_ready, mixT_mm,
         mixT_ready, o_mm, dve_done, pool_done, passed) = (sc.sem(n) for n in (
             "staged", "proj_mm", "qk_ready", "s_mm", "angle_ready", "cos_ready", "max_ready", "exp_ready",
             "mix_ready", "mixT_mm", "mixT_ready", "o_mm", "dve_done", "pool_done", "passed"))
        with nc.Block() as block:
            @block.gpsimd
            def _(pool):
                ch = Chain(pool, pool_done)
                with pool.If(pool.value_load(cos_is_one[:, :], min_val=0, max_val=1) < 1):
                    for w in (wqh, wkh):
                        ch.link(pool.memset(w[:, 0:1], 0.0))
                    with pool.Fori(0, HEADS) as n:
                        wait_apart(pool, o_mm, n * BT + BT, passed)
                        pool.tensor_copy(wqh[:, 1:1 + D], wq[:, ds(n % H * D, D)]).then_inc(staged, 1)
                        pool.tensor_copy(wkh[:, 1:1 + D], wk[:, ds(n % H * D, D)]).then_inc(staged, 1)
                        pool.tensor_copy(vh[:, :, :], V[:, ds(n // H * BT, BT), ds(n % H * D, D)]).then_inc(staged, 1)
                    pool.nop()

            @block.tensor
            def _(pe):
                with pe.If(pe.value_load(cos_is_one[:, :], min_val=0, max_val=1) < 1):
                    pe.sem_inc(o_mm, BT)
                    with pe.Fori(0, HEADS) as n:
                        for j, w in enumerate((wqh, wkh)):
                            if j:
                                pe.wait_ge(qk_ready, n * 2 + 1)
                            wait_apart(pe, staged, n * 3 + 3, passed)
                            for half in range(2):
                                ins = pe.matmul(proj[0:1 + D, half * BLK:(half + 1) * BLK], w[:, :],
                                                xT[:, ds(n // H * SEQ + half * BLK, BLK)], start=True, stop=True)
                            ins.then_inc(proj_mm, 1)
                        pe.wait_ge(qk_ready, n * 2 + 2)
                        for i in range(BT):
                            for half in range(2):
                                ins = pe.matmul(s_ps[:, half * BLK:(half + 1) * BLK], Q[:, i * P:(i + 1) * P],
                                                K[:, half * BLK:(half + 1) * BLK], start=True, stop=True)
                            ins.then_inc(s_mm, 1)
                            pe.wait_ge(mix_ready, n * BT + i + 1)
                            for k in range(BT):
                                ins = pe.transpose(mixT_ps[:, k * P:(k + 1) * P], mix[:, k * P:(k + 1) * P],
                                                   ident[:, :])
                            ins.then_inc(mixT_mm, 1)
                            pe.wait_ge(mixT_ready, n * BT + i + 1)
                            for k in range(BT):
                                ins = pe.matmul(o_ps[:, :], mixT[:, k * P:(k + 1) * P], vh[:, k, :],
                                                start=(k == 0), stop=(k == BT - 1))
                            ins.then_inc(o_mm, 1)
                    pe.nop()

            @block.scalar
            def _(act):
                with act.If(act.value_load(cos_is_one[:, :], min_val=0, max_val=1) < 1):
                    with act.Fori(0, HEADS) as n:
                        for i in range(BT):
                            with act.Fori(0, WL) as w:
                                step = (n * BT + i) * WL + w + 1
                                act.wait_ge(angle_ready, step)
                                act.activation(cosine[:, :], angle[:, :], ACT.Sin).then_inc(cos_ready, 1)
                                act.wait_ge(max_ready, step)
                                act.activation(ex[:, :], s[:, :], ACT.Exp, bias=neg_max[:, :],
                                               accum_out=den[:, :]).then_inc(exp_ready, 1)
                            act.wait_ge(mixT_mm, n * BT + i + 1)
                            act.copy(mixT[:, :], mixT_ps[:, :]).then_inc(mixT_ready, 1)
                    act.nop()

            @block.vector
            def _(v):
                ch = Chain(v, dve_done)
                TURN = 13
                with v.If(v.value_load(cos_is_one[:, :], min_val=0, max_val=1) < 1):
                    with ch.loop(HEADS, BT * (TURN * WL + 3) + 1) as n:
                        for j, (dst, bias) in enumerate(((Q, bqh), (K, bkh))):
                            v.wait_ge(proj_mm, n * 2 + j + 1)
                            v.tensor_scalar(dst[:, :], proj[0:1 + D, :], bias[:, ds(n % H, 1)], None,
                                            ALU.add).then_inc(qk_ready, 1)
                        for i in range(BT):
                            v.wait_ge(s_mm, n * BT + i + 1)
                            ch.link(v.tensor_copy(qk[:, :], s_ps[:, :]))
                            ch.link(v.memset(mix[:, :], 0.0))
                            v.sem_inc(passed, 1)
                            with ch.loop(WL, TURN) as w:
                                step = (n * BT + i) * WL + w + 1
                                ch.link(v.tensor_scalar(s[:, :], qk[:, :], scale_w[:, ds(w * H + n % H, 1)], None,
                                                        ALU.mult))
                                ch.link(v.scalar_tensor_tensor(out=arg[:, :], in0=s[:, :], scalar=KERR, in1=s[:, :],
                                                               op0=ALU.mult, op1=ALU.mult))
                                ch.link(v.tensor_scalar(turns[:, :], arg[:, :], 1.0 / (2 * float(np.pi)), ROUND,
                                                        ALU.mult, ALU.add))
                                ch.link(v.tensor_scalar(turns[:, :], turns[:, :], ROUND, None, ALU.subtract))
                                for part in (TWO_PI_A, TWO_PI_B, TWO_PI_C):
                                    ch.link(v.scalar_tensor_tensor(out=arg[:, :], in0=turns[:, :], scalar=-part,
                                                                   in1=arg[:, :], op0=ALU.mult, op1=ALU.add))
                                ch.link(v.scalar_tensor_tensor(out=turns[:, :], in0=arg[:, :], scalar=-1.0,
                                                               in1=arg[:, :], op0=ALU.mult, op1=ALU.max))
                                ch.link(v.tensor_scalar(turns[:, :], turns[:, :], float(np.pi), None, ALU.min))
                                v.tensor_scalar(angle[:, :], turns[:, :], -1.0, HALF_PI, ALU.mult,
                                                ALU.add).then_inc(angle_ready, 1)
                                v.wait_ge(cos_ready, step)
                                ch.link(v.tensor_tensor(s[:, :], s[:, :], cosine[:, :], ALU.mult))
                                v.tensor_reduce(neg_max[:, :], s[:, :], AX.X, ALU.max,
                                                negate=True).then_inc(max_ready, 1)
                                v.wait_ge(exp_ready, step)
                                ch.link(v.reciprocal(den[:, :], den[:, :]))
                                ch.link(v.tensor_tensor(den[:, :], den[:, :], share_w[:, ds(w, 1)], ALU.mult))
                                ch.link(v.scalar_tensor_tensor(out=mix[:, :], in0=ex[:, :], scalar=den[:, :],
                                                               in1=mix[:, :], op0=ALU.mult, op1=ALU.add))
                            v.sem_inc(mix_ready, 1)
                            v.wait_ge(o_mm, n * BT + i + 1 + BT)
                            ch.link(v.tensor_copy(heads[:, i, :], o_ps[:, :]))
                        ch.link(v.tensor_copy(V[:, ds(n // H * BT, BT), ds(n % H * D, D)], heads[:, :, :]))
                    v.nop()


def att_out(nc, x, ident, V, wo):
    with Scope(nc) as sc:
        turned_ps = [sc.ps(f"turned_ps{i}", [P, BLK]) for i in range(2)]
        out_ps = [sc.ps(f"out_ps{i}", [P, TPB, P]) for i in range(2)]
        turned = sc.sb("turned", [P, 2, BLK])
        turned_mm, turned_ready, out_ready, x_added = (
            sc.sem(n) for n in ("turned_mm", "turned_ready", "out_ready", "x_added"))
        with nc.Block() as block:
            @block.tensor
            def _(pe):
                for i in range(BLKS + 1):
                    if i < BLKS:
                        if i >= 2:
                            pe.wait_ge(turned_ready, i - 1)
                        for t in range(TPB):
                            ins = pe.transpose(turned_ps[i % 2][:, t * P:(t + 1) * P], V[:, i * TPB + t, :],
                                               ident[:, :])
                        ins.then_inc(turned_mm, 1)
                    if i:
                        k = i - 1
                        pe.wait_ge(turned_ready, k + 1)
                        if k >= 2:
                            pe.wait_ge(x_added, k - 1)
                        for t in range(TPB):
                            ins = pe.matmul(out_ps[k % 2][:, t, :], turned[:, k % 2, t * P:(t + 1) * P], wo[:, :],
                                            start=True, stop=True)
                        ins.then_inc(out_ready, 1)

            @block.scalar
            def _(act):
                for i in range(BLKS):
                    act.wait_ge(turned_mm, i + 1)
                    if i >= 2:
                        act.wait_ge(out_ready, i - 1)
                    act.copy(turned[:, i % 2, :], turned_ps[i % 2][:, :]).then_inc(turned_ready, 1)

            @block.vector
            def _(v):
                for i in range(BLKS):
                    v.wait_ge(out_ready, i + 1)
                    part = x[:, i * TPB:(i + 1) * TPB, :]
                    v.tensor_tensor(part, part, out_ps[i % 2][:, :, :], ALU.add).then_inc(x_added, 1)


def macaron(nc, out, L0_attn_x, L0_attn_W_in, L0_attn_W_conv, L0_attn_W_x, L0_attn_W_dt, L0_attn_b_dt, L0_attn_A_log,
            L0_attn_D_param, L0_attn_W_out, L0_ffn_w_router, L0_ffn_w1_stack, L0_ffn_w2_stack, L0_ffn_ws1, L0_ffn_ws2,
            L1_attn_Wq, L1_attn_bq, L1_attn_Wk, L1_attn_bk, L1_attn_Wv, L1_attn_bv, L1_attn_Wo, L1_attn_bo,
            L1_attn_phase_modulators, L1_attn_interference_weights, L1_ffn_gate_w, L1_ffn_w1, L1_ffn_b1, L1_ffn_w2,
            L1_ffn_b2, stages="fsfgag"):
    with Scope(nc) as sc:
        x, ident = sc.sb("x", [P, TILES, P]), sc.sb("ident", [P, P])
        make_identity(nc, ident)
        load_tokens(nc, L0_attn_x, x)
        for stage in stages:
            if stage == "f":
                ffn0(nc, x, ident, L0_ffn_w_router, L0_ffn_w1_stack, L0_ffn_w2_stack, L0_ffn_ws1, L0_ffn_ws2)
            if stage == "g":
                ffn1(nc, x, ident, L1_ffn_gate_w, L1_ffn_w1, L1_ffn_b1, L1_ffn_w2, L1_ffn_b2)
            if stage == "s":
                s6(nc, x, ident, L0_attn_W_in, L0_attn_W_conv, L0_attn_W_x, L0_attn_W_dt, L0_attn_b_dt,
                   L0_attn_A_log, L0_attn_D_param, L0_attn_W_out)
            if stage == "a":
                attention(nc, x, ident, L1_attn_Wq, L1_attn_bq, L1_attn_Wk, L1_attn_bk, L1_attn_Wv, L1_attn_bv,
                          L1_attn_Wo, L1_attn_bo, L1_attn_phase_modulators, L1_attn_interference_weights)
        store_tokens(nc, x, out)


_INS = ["L0_attn_x", "L0_attn_W_in", "L0_attn_W_conv", "L0_attn_W_x", "L0_attn_W_dt", "L0_attn_b_dt", "L0_attn_A_log",
        "L0_attn_D_param", "L0_attn_W_out", "L0_ffn_w_router", "L0_ffn_w1_stack", "L0_ffn_w2_stack", "L0_ffn_ws1",
        "L0_ffn_ws2", "L1_attn_Wq", "L1_attn_bq", "L1_attn_Wk", "L1_attn_bk", "L1_attn_Wv", "L1_attn_bv",
        "L1_attn_Wo", "L1_attn_bo", "L1_attn_phase_modulators", "L1_attn_interference_weights", "L1_ffn_gate_w",
        "L1_ffn_w1", "L1_ffn_b1", "L1_ffn_w2", "L1_ffn_b2"]


def kernel(**inputs):
    import numpy as _np
    import concourse.bacc as _bacc
    from concourse import mybir as _mybir
    from concourse.bass_utils import run_bass_kernel_spmd as _run

    nc = _bacc.Bacc("TRN2", target_bir_lowering=False, num_devices=1)
    arrays, args = {}, {}
    for name in _INS:
        a = _np.ascontiguousarray(inputs[name])
        arrays[f"in_{name}_dram"] = a
        args[name] = nc.dram_tensor(f"in_{name}_dram", a.shape, _mybir.dt.from_np(a.dtype), kind="ExternalInput").ap()
    out = nc.dram_tensor("out_0_dram", (BATCHES, SEQ, P), F32, kind="ExternalOutput").ap()
    macaron(nc, out, **args)
    r = _run(nc, [arrays], core_ids=[0])
    return r.results[0]["out_0_dram"]
```
